# Optimizing a Trainium2 kernel written in Bass

```python
import numpy as np
import jax
import jax.numpy as jnp

def _softmax(x, axis=-1):
    return jax.nn.softmax(x, axis=axis)

def _gelu(x):
    return jax.nn.gelu(x, approximate=True)

def _silu(x):
    return jax.nn.silu(x)

def _sigmoid(x):
    return jax.nn.sigmoid(x)

def _layernorm(x, axis=-1, eps=1e-05):
    m = jnp.mean(x, axis=axis, keepdims=True)
    v = jnp.var(x, axis=axis, keepdims=True)
    return (x - m) / jnp.sqrt(v + eps)

def _scatter_add(tgt, idx, src, axis=0):
    return tgt.at[idx].add(src)

def _segment_sum(src, seg, n):
    return jax.ops.segment_sum(src, seg, n)
kernel_name = 'mk_gnn_preln_d2_gnn_r8_92948c'

def setup_inputs(seed: int=0):
    np.random.seed(seed)
    _w = jnp.asarray

    def _rec_inputs():
        import jax
        import jax.numpy as jnp
        _gk = jax.random.key(seed)
        x = -0.0009044 + 1 * jax.random.normal(jax.random.fold_in(_gk, 1), (12500, 32), jnp.float32)
        src = jax.random.randint(jax.random.fold_in(_gk, 2), (400000,), 0, 12500, jnp.int32)
        dst = jnp.minimum((12500 * jax.random.uniform(jax.random.fold_in(_gk, 3), (400000,)) ** 2.0).astype(jnp.int32), 99999)
        _o = jnp.argsort(dst, stable=True)
        src = src[_o]
        dst = dst[_o]
        edge_attr_16 = 0.000196303 + 1.00016 * jax.random.normal(jax.random.fold_in(_gk, 12), (400000, 16), jnp.float32)
        edge_attr_32 = -9.77346e-05 + 0.999888 * jax.random.normal(jax.random.fold_in(_gk, 13), (400000, 32), jnp.float32)
        return (x, src, dst, edge_attr_16, edge_attr_32)
    x, src, dst, edge_attr_16, edge_attr_32 = _rec_inputs()

    def _L0_gnn_setup():
        import jax, jax.numpy as jnp
        import numpy as np
        N = 6250
        E = 200000
        DN = 32
        DE = 16
        DI = DN + DE
        DH = 2 * DI

        def _linear_params(key, fan_in, fan_out, dtype=jnp.float32):
            k1, k2 = jax.random.split(key)
            bound = 1.0 / np.sqrt(fan_in)
            w = jax.random.uniform(k1, (fan_in, fan_out), dtype, -bound, bound)
            b = jax.random.uniform(k2, (fan_out,), dtype, -bound, bound)
            return (w, b)
        key = jax.random.key(seed)
        ks = jax.random.split(key, 7)
        x = jax.random.normal(ks[0], (N, DN), dtype=jnp.float32)
        edge_index = jax.random.randint(ks[1], (2, E), 0, N, dtype=jnp.int64)
        edge_attr = jax.random.normal(ks[2], (E, DE), dtype=jnp.float32)
        w1a, b1a = _linear_params(ks[3], DI, DH)
        w1b, b1b = _linear_params(ks[4], DH, DH)
        w2a, b2a = _linear_params(ks[5], DN + DH, DI)
        w2b, b2b = _linear_params(ks[6], DI, DN)
        return {'x': x, 'edge_index': edge_index, 'edge_attr': edge_attr, 'w1a': w1a, 'b1a': b1a, 'w1b': w1b, 'b1b': b1b, 'w2a': w2a, 'b2a': b2a, 'w2b': w2b, 'b2b': b2b}
    _L0_gnn_all = _L0_gnn_setup()
    _L0_gnn_in = {k: v for k, v in _L0_gnn_all.items() if k in ('w1a', 'b1a', 'w1b', 'b1b', 'w2a', 'b2a', 'w2b', 'b2b')}
    del _L0_gnn_all

    def _L1_gnn_setup():
        import jax, jax.numpy as jnp
        import numpy as np
        N_NODES = 6250
        N_EDGES = 200000
        D_FEAT = 32
        key = jax.random.key(seed)
        k1, k2, k3, k4 = jax.random.split(key, 4)
        node_feat = jax.random.normal(k1, (N_NODES, D_FEAT), dtype=jnp.float32)
        edge_feat = jax.random.normal(k2, (N_EDGES, D_FEAT), dtype=jnp.float32)
        eps = jnp.zeros((1,), dtype=jnp.float32)
        src = jax.random.randint(k3, (N_EDGES,), 0, N_NODES, dtype=jnp.int64)
        dst = jax.random.randint(k4, (N_EDGES,), 0, N_NODES, dtype=jnp.int64)
        return {'node_feat': node_feat, 'edge_feat': edge_feat, 'eps': eps, 'src': src, 'dst': dst}
    _L1_gnn_all = _L1_gnn_setup()
    _L1_gnn_in = {k: v for k, v in _L1_gnn_all.items() if k in ('eps',)}
    del _L1_gnn_all
    return {'x': x, 'src': src, 'dst': dst, 'edge_attr_16': edge_attr_16, 'edge_attr_32': edge_attr_32, 'L0_gnn_w1a': _L0_gnn_in['w1a'], 'L0_gnn_b1a': _L0_gnn_in['b1a'], 'L0_gnn_w1b': _L0_gnn_in['w1b'], 'L0_gnn_b1b': _L0_gnn_in['b1b'], 'L0_gnn_w2a': _L0_gnn_in['w2a'], 'L0_gnn_b2a': _L0_gnn_in['b2a'], 'L0_gnn_w2b': _L0_gnn_in['w2b'], 'L0_gnn_b2b': _L0_gnn_in['b2b'], 'L1_gnn_eps': _L1_gnn_in['eps']}

def reference(x, src, dst, edge_attr_16, edge_attr_32, L0_gnn_w1a, L0_gnn_b1a, L0_gnn_w1b, L0_gnn_b1b, L0_gnn_w2a, L0_gnn_b2a, L0_gnn_w2b, L0_gnn_b2b, L1_gnn_eps):
    import jax
    import jax.numpy as jnp

    def _L0_gnn_ref(x, edge_index, edge_attr, w1a, b1a, w1b, b1b, w2a, b2a, w2b, b2b):
        import jax, jax.numpy as jnp
        import numpy as np
        N = 6250
        E = 200000
        DN = 32
        DE = 16
        DI = DN + DE
        DH = 2 * DI

        def _linear_params(key, fan_in, fan_out, dtype=jnp.float32):
            k1, k2 = jax.random.split(key)
            bound = 1.0 / np.sqrt(fan_in)
            w = jax.random.uniform(k1, (fan_in, fan_out), dtype, -bound, bound)
            b = jax.random.uniform(k2, (fan_out,), dtype, -bound, bound)
            return (w, b)
        row = edge_index[0]
        col = edge_index[1]
        h = jnp.concatenate([x[row], edge_attr], axis=1)
        h = jnp.maximum(h @ w1a + b1a, 0.0)
        h = h @ w1b + b1b
        s = jax.ops.segment_sum(h, col, num_segments=x.shape[0])
        cnt = jax.ops.segment_sum(jnp.ones((col.shape[0],), x.dtype), col, num_segments=x.shape[0])
        agg = s / jnp.maximum(cnt, 1.0)[:, None]
        h2 = jnp.concatenate([x, agg], axis=1)
        h2 = jnp.maximum(h2 @ w2a + b2a, 0.0)
        return h2 @ w2b + b2b

    def _L1_gnn_ref(node_feat, edge_feat, eps, src, dst):
        import jax, jax.numpy as jnp
        import numpy as np
        N_NODES = 6250
        N_EDGES = 200000
        D_FEAT = 32
        m = jax.nn.relu(node_feat[src] + edge_feat)
        neigh = jax.ops.segment_sum(m, dst, num_segments=node_feat.shape[0])
        return (1.0 + eps[0]) * node_feat + neigh
    edge_index = jnp.stack([src, dst])
    h = jnp.maximum(_layernorm(x, axis=-1), 0.0)
    x = x + _L0_gnn_ref(h, edge_index, edge_attr_16, L0_gnn_w1a, L0_gnn_b1a, L0_gnn_w1b, L0_gnn_b1b, L0_gnn_w2a, L0_gnn_b2a, L0_gnn_w2b, L0_gnn_b2b)
    h = jnp.maximum(_layernorm(x, axis=-1), 0.0)
    x = x + _L1_gnn_ref(h, edge_attr_32, L1_gnn_eps, src, dst)
    return x

_drawn_inputs = setup_inputs


def setup_inputs(seed=0):
    import zlib

    import numpy as np

    out = dict(_drawn_inputs(seed))
    spreads = {}
    factors = {'edge_attr_16': 8.0,
     'L0_gnn_w1a': 8.0,
     'L0_gnn_b1a': 33.149,
     'L0_gnn_w1b': 6.31,
     'L0_gnn_b1b': 51.679,
     'L0_gnn_b2a': 30.821,
     'L0_gnn_b2b': 7.765}
    for name, (base, spread) in spreads.items():
        noise = np.random.default_rng([zlib.crc32(name.encode()), seed]).standard_normal(out[name].shape)
        drawn = base * np.exp(spread * noise) if base else spread * noise
        out[name] = jnp.asarray(drawn.astype(out[name].dtype))
    for name, factor in factors.items():
        out[name] = (out[name] * factor).astype(out[name].dtype)
    return out
```

```python
from contextlib import ExitStack

import concourse.bass as bass
from concourse import mybir

P = 128
WINDOW = 64
WINDOW_BITS = 6
TILES = 5
CHUNK = TILES * P
SLOTS = 5
ROW_PAD = 8
LN_EPS = 1e-5

F32 = mybir.dt.float32
I32 = mybir.dt.int32
U32 = mybir.dt.uint32
ALU = mybir.AluOpType
ACT = mybir.ActivationFunctionType
AX = mybir.AxisListType
ENGINES = (mybir.EngineType.Pool, mybir.EngineType.Activation, mybir.EngineType.PE,
           mybir.EngineType.DVE, mybir.EngineType.SP)


def spread(ap, count, axis):
    shape = list(ap.shape)
    shape.insert(axis, count)
    return ap.unsqueeze(axis).broadcast_to(shape)


def gnn_kernel(nc, x, src_cols, dst_cols, dst_rows, edge16, edge32, w1a, b1a, w1b_t, b1b,
               w2a, b2a, w2b, b2b, eps, out):
    N, D = x.shape
    D_EDGE = edge16.shape[1]
    CHUNKS = edge16.shape[0]
    H1 = b1a.shape[0]
    H2 = b2a.shape[0]
    NP = 125
    BLOCKS = N // NP
    ITERS = CHUNKS // SLOTS
    SUMS = H1 + 1
    H2C = H2 + 1
    R_PAD = 64
    PSUM_COLS = 512

    LN_BLOCKS = 20
    LN_STEPS = BLOCKS // LN_BLOCKS
    GROUP = P // D
    GROUPS = BLOCKS // GROUP
    BATCH = 10
    BATCHES = BLOCKS // BATCH
    PAIRS = BATCH // 2
    assert NP * BLOCKS == N and ITERS * SLOTS == CHUNKS and LN_BLOCKS * LN_STEPS == BLOCKS
    assert GROUP * GROUPS == BLOCKS and BATCH * BATCHES == BLOCKS and LN_BLOCKS % BATCH == 0
    assert 1 << WINDOW_BITS == WINDOW and ITERS <= P and H2C <= R_PAD and BATCH * H2C <= PSUM_COLS

    projected_rows = nc.dram_tensor("projected_rows", [N, H1], F32, kind="Internal").ap()
    hidden_rows = nc.dram_tensor("hidden_rows", [N, D], F32, kind="Internal").ap()
    base_rows = nc.dram_tensor("base_rows", [ITERS, ROW_PAD], I32, kind="Internal").ap()
    base_line = nc.dram_tensor("base_line", [ITERS, SLOTS], F32, kind="Internal").ap()
    far_rows = nc.dram_tensor("far_rows", [ITERS, ROW_PAD], I32, kind="Internal").ap()

    with ExitStack() as ctx:
        def sb(name, shape, dt=F32):
            return ctx.enter_context(nc.sbuf_tensor(name, shape, dt))

        def sem(name):
            return ctx.enter_context(nc.semaphore(name))

        nodes = sb("nodes", [P, BLOCKS, D])
        hidden = sb("hidden", [P, BLOCKS, D])
        squares = sb("squares", [P, LN_BLOCKS, D])
        stats = sb("stats", [P, 4, BLOCKS])
        self_part = sb("self_part", [P, BLOCKS, H2])
        projected = sb("projected", [P, 2, GROUP, H1])
        hidden_t = sb("hidden_t", [P, 2, P])
        sums = sb("sums", [P, N + 2 * WINDOW])
        w_msg = sb("w_msg", [P, GROUP, H1])
        w_self = sb("w_self", [P, GROUP, H2])
        w_edge = sb("w_edge", [P, H1])
        w1b_ext_t = sb("w1b_ext_t", [P, SUMS])
        w2a_low = sb("w2a_low", [P, H2])
        w_mean = sb("w_mean", [P, H2C])
        w_out = sb("w_out", [P, 2, D])
        bias_msg = sb("bias_msg", [P, H1])
        bias_self = sb("bias_self", [P, H2])
        eps_col = sb("eps_col", [P, 1])
        one_eps = sb("one_eps", [P, 1])
        ln_eps = sb("ln_eps", [P, 1])
        ident = sb("ident", [P, P])
        window_i = sb("window_i", [P, WINDOW], I32)
        window_f = sb("window_f", [P, WINDOW])
        sources = sb("sources", [P, CHUNKS + SLOTS, TILES], I32)
        destinations = sb("destinations", [P, CHUNKS, TILES], I32)
        offsets = destinations[:, :, :].bitcast(F32)
        by_iter = sb("by_iter", [P, SLOTS, CHUNK], I32)
        low = sb("low", [P, SLOTS])
        high = sb("high", [P, SLOTS])
        low_i = sb("low_i", [P, ROW_PAD], I32)
        far_i = sb("far_i", [P, ROW_PAD], I32)
        far_n = sb("far_n", [P, ROW_PAD], I32)
        base_all = sb("base_all", [P, CHUNKS])
        bases = sb("bases", [1, ITERS * ROW_PAD], I32)
        fars = sb("fars", [1, ITERS * ROW_PAD], I32)
        far_max = sb("far_max", [1, 1])
        far_flag = sb("far_flag", [1, 1], I32)
        index = [sb(f"index{k}", [P, TILES], I32) for k in range(SLOTS)]
        edge_t = [sb(f"edge_t{k}", [D_EDGE, CHUNK]) for k in range(SLOTS)]
        edge_r = [sb(f"edge_r{k}", [P, TILES, D]) for k in range(SLOTS)]
        gathered = [sb(f"gathered{k}", [P, TILES, H1]) for k in range(SLOTS)]
        message = [sb(f"message{k}", [P, TILES, SUMS]) for k in range(SLOTS)]
        onehot = [sb(f"onehot{k}", [P, TILES, WINDOW]) for k in range(SLOTS)]
        far_offset = sb("far_offset", [P, TILES])
        inverse = sb("inverse", [P, 2, BATCH])
        update = sb("update", [P, 2, BATCH, R_PAD])
        update_t = sb("update_t", [P, 2, PAIRS, P])

        bank = [ctx.enter_context(nc.psum_tensor(f"bank{k}", [P, PSUM_COLS], F32)) for k in range(8)]

        x_view = x.rearrange("(p b) f -> p b f", b=BLOCKS)
        out_view = out.rearrange("(p b) f -> p b f", b=BLOCKS)
        projected_view = projected_rows.rearrange("(p b) f -> p b f", b=BLOCKS)
        hidden_view = hidden_rows.rearrange("(p b) f -> p b f", b=BLOCKS)

        def ln_blocks(step):
            return slice(step * LN_BLOCKS, (step + 1) * LN_BLOCKS)

        def norm_semaphores(layer):
            return {name: sem(f"{name}{layer}") for name in
                    ("totals", "averaged", "centred", "squared", "spreads", "rooted", "inverted", "normed")}

        def normalize(dve, step, s):
            b = ln_blocks(step)
            mean, total, inverse_root = stats[0:NP, 0, b], stats[0:NP, 1, b], stats[0:NP, 3, b]
            nc.vector.tensor_reduce(total, nodes[0:NP, b, :], AX.X, ALU.add).then_inc(s["totals"], 1)
            dve.wait_ge(s["totals"], step + 1)
            nc.vector.tensor_scalar(mean, total, 1.0 / D, None, ALU.mult).then_inc(s["averaged"], 1)
            dve.wait_ge(s["averaged"], step + 1)
            nc.vector.tensor_tensor(hidden[0:NP, b, :], nodes[0:NP, b, :], spread(mean, D, 2),
                                    ALU.subtract).then_inc(s["centred"], 1)
            dve.wait_ge(s["squared"], step + 1)
            nc.vector.tensor_reduce(total, squares[0:NP, :, :], AX.X, ALU.add).then_inc(s["spreads"], 1)
            dve.wait_ge(s["rooted"], step + 1)
            nc.vector.reciprocal(inverse_root, stats[0:NP, 2, b]).then_inc(s["inverted"], 1)
            dve.wait_ge(s["inverted"], step + 1)
            nc.vector.scalar_tensor_tensor(out=hidden[0:NP, b, :], in0=hidden[0:NP, b, :], scalar=0.0,
                                           in1=spread(inverse_root, D, 2), op0=ALU.max,
                                           op1=ALU.mult).then_inc(s["normed"], 1)

        def square_and_root(act, step, s):
            b = ln_blocks(step)
            act.wait_ge(s["centred"], step + 1)
            nc.scalar.activation(squares[0:NP, :, :], hidden[0:NP, b, :], ACT.Square).then_inc(s["squared"], 1)
            act.wait_ge(s["spreads"], step + 1)
            nc.scalar.activation(stats[0:NP, 2, b], stats[0:NP, 1, b], ACT.Sqrt, bias=ln_eps[0:NP, 0:1],
                                 scale=1.0 / D).then_inc(s["rooted"], 1)

        def prepare():
            x_in = sem("x_in")
            dst_in = sem("dst_in")
            src_in = sem("src_in")
            weights_in = sem("weights_in")
            diagonals_in = sem("diagonals_in")
            diagonals_clear = sem("diagonals_clear")
            ident_clear = sem("ident_clear")
            ident_ready = sem("ident_ready")
            counted = sem("counted")
            fills = sem("fills")
            tail_fills = sem("tail_fills")
            norm = norm_semaphores(0)
            normed = norm["normed"]
            bound_steps = sem("bound_steps")
            bounds_ready = sem("bounds_ready")
            bounds_out = sem("bounds_out")
            bounds_in = sem("bounds_in")
            farthest = sem("farthest")
            turned = sem("turned")
            turned_copied = sem("turned_copied")
            products = sem("products")
            added_msg = sem("added_msg")
            added_self = sem("added_self")
            rows_out = [sem("rows_out_even"), sem("rows_out_odd")]
            w_mean_made = sem("w_mean_made")
            ln_eps_ready = sem("ln_eps_ready")
            N_WEIGHTS = 7
            N_DIAGONALS = 2 * GROUP + 4

            with nc.Block() as block:
                @block.sync
                def _(sp):
                    sp.dma_start(nodes[0:NP, :, :], x_view).then_inc(x_in, 16)
                    sp.dma_start(by_iter[0:ITERS, :, :], dst_rows).then_inc(dst_in, 16)
                    sp.dma_start(destinations[:, :, :], dst_cols).then_inc(dst_in, 16)
                    sp.dma_start(sources[:, 0:CHUNKS, :], src_cols).then_inc(src_in, 16)
                    sp.wait_ge(bounds_ready, 3)
                    sp.dma_start(base_line, low[0:ITERS, :]).then_inc(bounds_out, 16)
                    sp.dma_start(base_rows, low_i[0:ITERS, :]).then_inc(bounds_out, 16)
                    sp.dma_start(far_rows, far_n[0:ITERS, :]).then_inc(bounds_out, 16)
                    sp.wait_ge(bounds_out, 48)
                    sp.dma_start(base_all[:, :], base_line.rearrange("i s -> (i s)").partition_broadcast(P)
                                 ).then_inc(bounds_in, 16)
                    sp.dma_start(bases[:, :], base_rows.rearrange("i s -> (i s)").unsqueeze(0)
                                 ).then_inc(bounds_in, 16)
                    sp.dma_start(fars[:, :], far_rows.rearrange("i s -> (i s)").unsqueeze(0)
                                 ).then_inc(bounds_in, 16)
                    for g in range(GROUPS):
                        sp.wait_ge(added_msg, g + 1)
                        sp.dma_start(projected_view[:, g * GROUP:(g + 1) * GROUP, :],
                                     projected[0:NP, g % 2, :, :]).then_inc(rows_out[g % 2], 16)
                    sp.wait_ge(rows_out[0], 16 * ((GROUPS + 1) // 2))
                    sp.wait_ge(rows_out[1], 16 * (GROUPS // 2))

                @block.scalar
                def _(act):
                    act.dma_start(bias_msg[:, :], b1a.partition_broadcast(P)).then_inc(weights_in, 16)
                    act.dma_start(bias_self[:, :], b2a.partition_broadcast(P)).then_inc(weights_in, 16)
                    act.dma_start(w_edge[0:D_EDGE, :], w1a[D:D + D_EDGE, :]).then_inc(weights_in, 16)
                    act.dma_start(w1b_ext_t[0:H1, 0:H1], w1b_t).then_inc(weights_in, 16)
                    act.dma_start(w1b_ext_t[0:H1, H1:SUMS], b1b.unsqueeze(1)).then_inc(weights_in, 16)
                    act.dma_start(w2a_low[0:H1, :], w2a[D:D + H1, :]).then_inc(weights_in, 16)
                    act.dma_start(eps_col[:, :], eps.partition_broadcast(P)).then_inc(weights_in, 16)
                    act.wait_ge(diagonals_clear, 3)
                    for j in range(GROUP):
                        act.dma_start(w_msg[j * D:(j + 1) * D, j, :], w1a[0:D, :]).then_inc(diagonals_in, 16)
                        act.dma_start(w_self[j * D:(j + 1) * D, j, :], w2a[0:D, :]).then_inc(diagonals_in, 16)
                    for j in range(2):
                        act.dma_start(w_out[j * R_PAD:j * R_PAD + H2, j, :], w2b).then_inc(diagonals_in, 16)
                        act.dma_start(w_out[j * R_PAD + H2:j * R_PAD + H2C, j, :],
                                      b2b.unsqueeze(0)).then_inc(diagonals_in, 16)
                    act.wait_ge(ln_eps_ready, 1)
                    for step in range(LN_STEPS):
                        square_and_root(act, step, norm)
                    for g in range(GROUPS):
                        act.wait_ge(turned, g + 1)
                        if g >= 2:
                            act.wait_ge(products, g - 1)
                        nc.scalar.copy(hidden_t[:, g % 2, 0:NP], bank[g % 2][:, 0:NP]).then_inc(turned_copied, 1)
                    act.wait_ge(weights_in, 16 * N_WEIGHTS)
                    act.wait_ge(diagonals_in, 16 * N_DIAGONALS)

                @block.gpsimd
                def _(pool):
                    nc.gpsimd.memset(w_msg[:, :, :], 0.0).then_inc(diagonals_clear, 1)
                    nc.gpsimd.memset(w_self[:, :, :], 0.0).then_inc(diagonals_clear, 1)
                    nc.gpsimd.memset(w_out[:, :, :], 0.0).then_inc(diagonals_clear, 1)
                    nc.gpsimd.memset(ident[:, :], 0.0).then_inc(ident_clear, 1)
                    pool.wait_ge(ident_clear, 1)
                    nc.gpsimd.affine_select(out=ident[:, :], in_=ident[:, :], compare_op=ALU.not_equal,
                                            fill=1.0, base=0, pattern=[[-1, P]],
                                            channel_multiplier=1).then_inc(ident_ready, 1)
                    nc.gpsimd.iota(window_i[:, :], pattern=[[1, WINDOW]], base=0,
                                   channel_multiplier=0).then_inc(counted, 1)
                    nc.gpsimd.memset(sources[:, CHUNKS:CHUNKS + SLOTS, :], 0).then_inc(fills, 1)
                    nc.gpsimd.memset(w_mean[:, :], 0.0).then_inc(fills, 1)
                    nc.gpsimd.memset(update[:, :, :, :], 0.0).then_inc(fills, 1)
                    pool.wait_ge(fills, 3)
                    nc.gpsimd.memset(update[:, :, :, H2:H2C], 1.0).then_inc(tail_fills, 1)
                    pool.wait_ge(tail_fills, 1)
                    nc.gpsimd.memset(w_mean[H1:SUMS, H2:H2C], 1.0).then_inc(tail_fills, 1)
                    pool.wait_ge(tail_fills, 2)
                    nc.gpsimd.memset(sums[:, :], 0.0).then_inc(tail_fills, 1)
                    for k in range(SLOTS):
                        nc.gpsimd.memset(message[k][:, :, H1:SUMS], 1.0).then_inc(tail_fills, 1)
                    pool.wait_ge(tail_fills, 3 + SLOTS)

                @block.tensor
                def _(pe):
                    pe.wait_ge(ident_ready, 1)

                    def turn(g):
                        pe.wait_ge(normed, (g + 1) * GROUP // LN_BLOCKS + (1 if (g + 1) * GROUP % LN_BLOCKS else 0))
                        if g >= 2:
                            pe.wait_ge(turned_copied, g - 1)
                        nc.tensor.transpose(bank[g % 2][:, 0:NP],
                                            hidden[0:NP, g * GROUP:(g + 1) * GROUP, :].rearrange("p b f -> p (b f)"),
                                            ident[0:NP, 0:NP]).then_inc(turned, 1)

                    turn(0)
                    for g in range(GROUPS):
                        if g + 1 < GROUPS:
                            turn(g + 1)
                        if g == 0:
                            pe.wait_ge(diagonals_in, 16 * N_DIAGONALS)
                        pe.wait_ge(turned_copied, g + 1)
                        if g >= 2:
                            pe.wait_ge(added_msg, g - 1)
                            pe.wait_ge(added_self, g - 1)
                        nc.tensor.matmul(bank[2 + g % 2][0:NP, 0:GROUP * H1], hidden_t[:, g % 2, 0:NP],
                                         w_msg[:, :, :].rearrange("p j n -> p (j n)"), start=True, stop=True)
                        nc.tensor.matmul(bank[4 + g % 2][0:NP, 0:GROUP * H2], hidden_t[:, g % 2, 0:NP],
                                         w_self[:, :, :].rearrange("p j n -> p (j n)"), start=True,
                                         stop=True).then_inc(products, 1)
                    pe.wait_ge(weights_in, 16 * N_WEIGHTS)
                    nc.tensor.matmul(bank[6][0:SUMS, 0:H2], w1b_ext_t[0:H1, :], w2a_low[0:H1, :], start=True,
                                     stop=True).then_inc(w_mean_made, 1)

                @block.vector
                def _(dve):
                    nc.vector.memset(ln_eps[:, :], LN_EPS).then_inc(ln_eps_ready, 1)
                    dve.wait_ge(x_in, 16)
                    normalize(dve, 0, norm)
                    nc.vector.memset(low_i[:, :], 0).then_inc(bound_steps, 1)
                    nc.vector.memset(far_n[:, :], 0).then_inc(bound_steps, 1)
                    dve.wait_ge(dst_in, 32)
                    nc.vector.tensor_reduce(low[0:ITERS, :], by_iter[0:ITERS, :, :], AX.X,
                                            ALU.min).then_inc(bounds_ready, 1)
                    nc.vector.tensor_reduce(high[0:ITERS, :], by_iter[0:ITERS, :, :], AX.X,
                                            ALU.max).then_inc(bound_steps, 1)
                    dve.wait_ge(bounds_ready, 1)
                    dve.wait_ge(bound_steps, 3)
                    nc.vector.tensor_copy(low_i[0:ITERS, 0:SLOTS], low[0:ITERS, :]).then_inc(bounds_ready, 1)
                    nc.vector.tensor_tensor(far_i[0:ITERS, 0:SLOTS], high[0:ITERS, :], low[0:ITERS, :],
                                            ALU.subtract).then_inc(bound_steps, 1)
                    dve.wait_ge(bound_steps, 4)
                    nc.vector.tensor_single_scalar(far_n[0:ITERS, 0:SLOTS], far_i[0:ITERS, 0:SLOTS],
                                                   WINDOW_BITS, ALU.arith_shift_right).then_inc(bounds_ready, 1)
                    for step in range(1, LN_STEPS):
                        normalize(dve, step, norm)
                    dve.wait_ge(weights_in, 16 * N_WEIGHTS)
                    for g in range(GROUPS):
                        dve.wait_ge(products, g + 1)
                        if g >= 2:
                            dve.wait_ge(rows_out[g % 2], 16 * (g // 2))
                        nc.vector.tensor_tensor(projected[0:NP, g % 2, :, :],
                                                bank[2 + g % 2][0:NP, 0:GROUP * H1].rearrange("p (j n) -> p j n", n=H1),
                                                spread(bias_msg[0:NP, :], GROUP, 1), ALU.add).then_inc(added_msg, 1)
                        nc.vector.tensor_tensor(self_part[0:NP, g * GROUP:(g + 1) * GROUP, :],
                                                bank[4 + g % 2][0:NP, 0:GROUP * H2].rearrange("p (j n) -> p j n", n=H2),
                                                spread(bias_self[0:NP, :], GROUP, 1), ALU.add).then_inc(added_self, 1)
                    dve.wait_ge(bounds_in, 48)
                    nc.vector.tensor_tensor(offsets, destinations[:, :, :],
                                            spread(base_all[:, :], TILES, 2), ALU.subtract)
                    nc.vector.tensor_reduce(far_max[:, :], fars[:, :], AX.X, ALU.max).then_inc(farthest, 1)
                    dve.wait_ge(counted, 1)
                    nc.vector.tensor_copy(window_f[:, :], window_i[:, :])
                    dve.wait_ge(farthest, 1)
                    nc.vector.tensor_copy(far_flag[:, :], far_max[:, :])
                    dve.wait_ge(src_in, 16)
                    stage_first_round()
                    nc.vector.tensor_scalar(one_eps[:, :], eps_col[:, :], 1.0, None, ALU.add)
                    dve.wait_ge(w_mean_made, 1)
                    dve.wait_ge(fills, 3)
                    nc.vector.tensor_copy(w_mean[0:SUMS, 0:H2], bank[6][0:SUMS, 0:H2])

        def stage_first_round():
            for k in range(SLOTS):
                nc.vector.tensor_copy(index[k][:, :], sources[:, k, :])

        def gathered_rows(k, row):
            flat = gathered[k][:, :, :].rearrange("p t n -> p (t n)")[:, 0:TILES * row]
            return flat.rearrange("p (t n) -> p t n", n=row)

        def sum_near_windows(layer):
            width, row, table = (SUMS, H1, projected_rows) if layer == 0 else (D, D, hidden_rows)
            index_ready = sem(f"index_ready{layer}")
            edge_in = [sem(f"edge_in{layer}_{k}") for k in range(SLOTS)]
            gather_in = [sem(f"gather_in{layer}_{k}") for k in range(SLOTS)]
            multiplied = sem(f"multiplied{layer}")
            added = sem(f"added{layer}")
            rectified = sem(f"rectified{layer}")
            hot = sem(f"hot{layer}")
            windows = sem(f"windows{layer}")
            summed = sem(f"summed{layer}")
            opened = sem(f"opened{layer}")
            edges_used = multiplied if layer == 0 else added

            with nc.Block() as block:
                @block.sync
                def _(sp):
                    with sp.Fori(0, ITERS) as i:
                        for k in range(SLOTS):
                            sp.wait_ge(edges_used, SLOTS * i + (k + 1))
                            if layer == 0:
                                sp.dma_start(edge_t[k][:, :], edge16[bass.ds(SLOTS * i + k, 1), :, :].rearrange(
                                    "o d e -> (o d) e")).then_inc(edge_in[k], 16)
                            else:
                                sp.dma_start(edge_r[k][:, :, :],
                                             edge32[bass.ds(SLOTS * i + k, 1), :, :, :].rearrange(
                                                 "o p t d -> (o p) t d")).then_inc(edge_in[k], 16)

                @block.gpsimd
                def _(pool):
                    with pool.Fori(0, ITERS) as i:
                        for k in range(SLOTS):
                            pool.wait_ge(index_ready, SLOTS * i + (k + 1))
                            pool.wait_ge(rectified, SLOTS * i + (k + 1))
                            pool.sem_inc(opened, 1)
                            for t in range(TILES):
                                pool.indirect_dma_start(
                                    gathered_rows(k, row)[:, t, :], None, table,
                                    bass.IndirectOffsetOnAxis(ap=index[k][:, t:t + 1], axis=0)
                                ).then_inc(gather_in[k], 16)

                @block.tensor
                def _(pe):
                    if layer == 0:
                        pe.sem_inc(multiplied, SLOTS)
                    pe.sem_inc(windows, SLOTS)
                    with pe.Fori(0, ITERS) as i:
                        def edge_products(k):
                            pe.wait_ge(edge_in[k], 16 * i + 16)
                            pe.wait_ge(added, SLOTS * i + (k + SLOTS - 1))
                            for t in range(TILES):
                                last = nc.tensor.matmul(bank[k % 3][:, t * H1:(t + 1) * H1],
                                                        edge_t[k][:, t * P:(t + 1) * P],
                                                        w_edge[0:D_EDGE, :], start=True, stop=True)
                            last.then_inc(multiplied, 1)

                        if layer == 0:
                            edge_products(0)
                        for k in range(SLOTS):
                            if layer == 0 and k + 1 < SLOTS:
                                edge_products(k + 1)
                            pe.wait_ge(rectified, SLOTS * i + (k + SLOTS + 1))
                            pe.wait_ge(hot, SLOTS * i + (k + 1))
                            pe.wait_ge(summed, SLOTS * i + (k + 1))
                            for t in range(TILES):
                                last = nc.tensor.matmul(bank[3 + k % 3][0:width, 0:WINDOW],
                                                        message[k][:, t, 0:width], onehot[k][:, t, :],
                                                        start=(t == 0), stop=(t == TILES - 1))
                            last.then_inc(windows, 1)

                @block.scalar
                def _(act):
                    act.sem_inc(rectified, SLOTS)
                    with act.Fori(0, ITERS) as i:
                        for k in range(SLOTS):
                            act.wait_ge(added, SLOTS * i + (k + SLOTS + 1))
                            act.wait_ge(windows, SLOTS * i + (k + 1))
                            nc.scalar.activation(message[k][:, :, 0:row], gathered_rows(k, row),
                                                 ACT.Relu).then_inc(rectified, 1)

                @block.vector
                def _(dve):
                    dve.sem_inc(added, SLOTS)
                    dve.sem_inc(summed, 2)
                    dve.sem_inc(index_ready, SLOTS)
                    with dve.Fori(0, ITERS) as i:
                        def add_window(k, base):
                            dve.wait_ge(windows, SLOTS * i + (k + SLOTS + 1))
                            dve.wait_ge(summed, SLOTS * i + (k + 2))
                            nc.vector.tensor_tensor(sums[0:width, bass.ds(base, WINDOW)],
                                                    sums[0:width, bass.ds(base, WINDOW)],
                                                    bank[3 + k % 3][0:width, 0:WINDOW],
                                                    ALU.add).then_inc(summed, 1)

                        base_of = []
                        for k in range(SLOTS):
                            base_of.append(dve.value_load(bases[0:1, bass.ds(ROW_PAD * i + k, 1)], min_val=0,
                                                          max_val=N - 1))
                            dve.wait_ge(windows, SLOTS * i + (k + 1))
                            nc.vector.tensor_tensor(
                                onehot[k][:, :, :], spread(window_f[:, :], TILES, 1),
                                spread(offsets[:, bass.ds(SLOTS * i + k, 1), :].rearrange("p o t -> p (o t)"),
                                       WINDOW, 2), ALU.is_equal).then_inc(hot, 1)
                            dve.wait_ge(gather_in[k], 16 * TILES * i + 16 * TILES)
                            if layer == 0:
                                dve.wait_ge(multiplied, SLOTS * i + (k + SLOTS + 1))
                                other = bank[k % 3][:, 0:TILES * H1].rearrange("p (t n) -> p t n", n=H1)
                            else:
                                dve.wait_ge(edge_in[k], 16 * i + 16)
                                other = edge_r[k][:, :, :]
                            nc.vector.tensor_tensor(gathered_rows(k, row), gathered_rows(k, row), other,
                                                    ALU.add).then_inc(added, 1)
                            nc.vector.tensor_copy(
                                index[k][:, :],
                                sources[:, bass.ds(SLOTS * i + (k + SLOTS), 1), :].rearrange("p o t -> p (o t)")
                            ).then_inc(index_ready, 1)
                            if k:
                                add_window(k - 1, base_of[k - 1])
                        add_window(SLOTS - 1, base_of[SLOTS - 1])

        def sum_far_windows(layer):
            width, row, table = (SUMS, H1, projected_rows) if layer == 0 else (D, D, hidden_rows)
            staged = sem(f"far_staged{layer}")
            edge_in = sem(f"far_edge_in{layer}")
            gather_in = [sem(f"far_gather_in{layer}_{k}") for k in range(SLOTS)]
            multiplied = sem(f"far_multiplied{layer}")
            added = sem(f"far_added{layer}")
            moved = sem(f"far_moved{layer}")
            hot = sem(f"far_hot{layer}")
            window = sem(f"far_window{layer}")

            def clear(*used):
                for s in used:
                    nc.sync.sem_clear(s)
                nc.all_engine_barrier()

            def chunk_messages(i, k):
                chunk = SLOTS * i + k

                with nc.Block() as block:
                    @block.sync
                    def _(sp):
                        if layer == 0:
                            sp.dma_start(edge_t[0][:, :], edge16[bass.ds(chunk, 1), :, :].rearrange(
                                "o d e -> (o d) e")).then_inc(edge_in, 16)
                        else:
                            sp.dma_start(edge_r[0][:, :, :], edge32[bass.ds(chunk, 1), :, :, :].rearrange(
                                "o p t d -> (o p) t d")).then_inc(edge_in, 16)

                    @block.gpsimd
                    def _(pool):
                        pool.wait_ge(staged, 1)
                        for t in range(TILES):
                            pool.indirect_dma_start(
                                gathered_rows(0, row)[:, t, :], None, table,
                                bass.IndirectOffsetOnAxis(ap=index[0][:, t:t + 1], axis=0)
                            ).then_inc(gather_in[k], 16)

                    @block.tensor
                    def _(pe):
                        if layer == 0:
                            pe.wait_ge(edge_in, 16)
                            for t in range(TILES):
                                last = nc.tensor.matmul(bank[0][:, t * H1:(t + 1) * H1],
                                                        edge_t[0][:, t * P:(t + 1) * P], w_edge[0:D_EDGE, :],
                                                        start=True, stop=True)
                            last.then_inc(multiplied, 1)

                    @block.scalar
                    def _(act):
                        act.wait_ge(added, 1)
                        nc.scalar.activation(message[0][:, :, 0:row], gathered_rows(0, row), ACT.Relu)

                    @block.vector
                    def _(dve):
                        nc.vector.tensor_copy(index[0][:, :], sources[:, bass.ds(chunk, 1), :].rearrange(
                            "p o t -> p (o t)")).then_inc(staged, 1)
                        nc.vector.tensor_copy(far_offset[:, :], offsets[:, bass.ds(chunk, 1), :].rearrange(
                            "p o t -> p (o t)"))
                        dve.wait_ge(gather_in[k], 16 * TILES * i + 16 * TILES)
                        if layer == 0:
                            dve.wait_ge(multiplied, 1)
                            other = bank[0][:, 0:TILES * H1].rearrange("p (t n) -> p t n", n=H1)
                        else:
                            dve.wait_ge(edge_in, 16)
                            other = edge_r[0][:, :, :]
                        nc.vector.tensor_tensor(gathered_rows(0, row), gathered_rows(0, row), other,
                                                ALU.add).then_inc(added, 1)
                clear(staged, edge_in, multiplied, added)

            def add_window(base, w):
                with nc.Block() as block:
                    @block.vector
                    def _(dve):
                        nc.vector.tensor_scalar(far_offset[:, :], far_offset[:, :], float(-WINDOW), None,
                                                ALU.add).then_inc(moved, 1)
                        dve.wait_ge(moved, 1)
                        nc.vector.tensor_tensor(onehot[0][:, :, :], spread(window_f[:, :], TILES, 1),
                                                spread(far_offset[:, :], WINDOW, 2), ALU.is_equal).then_inc(hot, 1)
                        dve.wait_ge(window, 1)
                        first = nc.s_assert_within(base + w * WINDOW, 0, N - 1 + WINDOW)
                        nc.vector.tensor_tensor(sums[0:width, bass.ds(first, WINDOW)],
                                                sums[0:width, bass.ds(first, WINDOW)],
                                                bank[3][0:width, 0:WINDOW], ALU.add)

                    @block.tensor
                    def _(pe):
                        pe.wait_ge(hot, 1)
                        for t in range(TILES):
                            last = nc.tensor.matmul(bank[3][0:width, 0:WINDOW], message[0][:, t, 0:width],
                                                    onehot[0][:, t, :], start=(t == 0), stop=(t == TILES - 1))
                        last.then_inc(window, 1)
                clear(moved, hot, window)

            some = nc.values_load(far_flag[0:1, 0:1], min_val=0, max_val=N)
            with nc.If(some > 0):
                with nc.Fori(0, ITERS) as i:
                    for k in range(SLOTS):
                        chunk_messages(i, k)
                        base = nc.values_load(bases[0:1, bass.ds(ROW_PAD * i + k, 1)], min_val=0, max_val=N - 1)
                        last = nc.values_load(fars[0:1, bass.ds(ROW_PAD * i + k, 1)], min_val=0,
                                              max_val=(N - 1) // WINDOW)
                        with nc.Fori(1, last + 1) as w:
                            add_window(base, w)

        def update_nodes():
            norm = norm_semaphores(1)
            normed = norm["normed"]
            means = sem("means")
            counts = sem("counts")
            scaled = sem("scaled")
            shifted = sem("shifted")
            updates = sem("updates")
            turned = sem("turned1")
            turned_copied = sem("turned_copied1")
            outputs = sem("outputs")
            advanced = sem("advanced")
            hidden_out = sem("hidden_out")
            cleared = sem("cleared")
            SPLIT = 3

            def blocks(q):
                return slice(q * BATCH, (q + 1) * BATCH)

            with nc.Block() as block:
                @block.tensor
                def _(pe):
                    def mean(q):
                        if q >= 2:
                            pe.wait_ge(scaled, q - 1)
                        for j in range(BATCH):
                            b = q * BATCH + j
                            last = nc.tensor.matmul(bank[q % 2][0:NP, j * H2C:(j + 1) * H2C],
                                                    sums[0:SUMS, b:N:BLOCKS], w_mean[0:SUMS, :],
                                                    start=True, stop=True)
                        last.then_inc(means, 1)

                    mean(0)
                    for q in range(BATCHES):
                        if q + 1 < BATCHES:
                            mean(q + 1)
                        pe.wait_ge(updates, q + 1)
                        if q >= 2:
                            pe.wait_ge(turned_copied, q - 1)
                        for j in range(PAIRS):
                            to = bank[2 + 2 * (q % 2) + j // SPLIT]
                            last = nc.tensor.transpose(
                                to[:, (j % SPLIT) * NP:(j % SPLIT + 1) * NP],
                                update[0:NP, q % 2, 2 * j:2 * j + 2, :].rearrange("p b f -> p (b f)"),
                                ident[0:NP, 0:NP])
                        last.then_inc(turned, 1)
                        pe.wait_ge(turned_copied, q + 1)
                        if q >= 2:
                            pe.wait_ge(advanced, q - 1)
                        for j in range(PAIRS):
                            last = nc.tensor.matmul(bank[6 + q % 2][0:NP, j * 2 * D:(j + 1) * 2 * D],
                                                    update_t[:, q % 2, j, 0:NP],
                                                    w_out[:, :, :].rearrange("p j n -> p (j n)"),
                                                    start=True, stop=True)
                        last.then_inc(outputs, 1)

                @block.scalar
                def _(act):
                    for q in range(BATCHES):
                        act.wait_ge(shifted, q + 1)
                        nc.scalar.activation(update[0:NP, q % 2, :, 0:H2], update[0:NP, q % 2, :, 0:H2],
                                             ACT.Relu).then_inc(updates, 1)
                        act.wait_ge(turned, q + 1)
                        if q >= 2:
                            act.wait_ge(outputs, q - 1)
                        nc.scalar.copy(update_t[:, q % 2, 0:SPLIT, 0:NP],
                                       bank[2 + 2 * (q % 2)][:, 0:SPLIT * NP].rearrange("p (j n) -> p j n", n=NP))
                        nc.scalar.copy(update_t[:, q % 2, SPLIT:PAIRS, 0:NP],
                                       bank[3 + 2 * (q % 2)][:, 0:(PAIRS - SPLIT) * NP].rearrange(
                                           "p (j n) -> p j n", n=NP)).then_inc(turned_copied, 1)
                        if (q + 1) * BATCH % LN_BLOCKS == 0:
                            square_and_root(act, (q + 1) * BATCH // LN_BLOCKS - 1, norm)

                @block.vector
                def _(dve):
                    def first_layer(q):
                        s = q % 2
                        dve.wait_ge(means, q + 1)
                        view = bank[s][0:NP, 0:BATCH * H2C].rearrange("p (b n) -> p b n", n=H2C)
                        count = view[:, :, H2:H2C].rearrange("p b o -> p (b o)")
                        nc.vector.tensor_scalar(inverse[0:NP, 0, :], count, 1.0, None, ALU.max).then_inc(counts, 1)
                        dve.wait_ge(counts, 2 * q + 1)
                        nc.vector.reciprocal(inverse[0:NP, 1, :], inverse[0:NP, 0, :]).then_inc(counts, 1)
                        dve.wait_ge(counts, 2 * q + 2)
                        if q >= 2:
                            dve.wait_ge(turned, q - 1)
                        nc.vector.tensor_tensor(update[0:NP, s, :, 0:H2], view[:, :, 0:H2],
                                                spread(inverse[0:NP, 1, :], H2, 2), ALU.mult).then_inc(scaled, 1)
                        dve.wait_ge(scaled, q + 1)
                        nc.vector.tensor_tensor(update[0:NP, s, :, 0:H2], update[0:NP, s, :, 0:H2],
                                                self_part[0:NP, blocks(q), :], ALU.add).then_inc(shifted, 1)

                    stage_first_round()
                    first_layer(0)
                    for q in range(BATCHES):
                        if q + 1 < BATCHES:
                            first_layer(q + 1)
                        dve.wait_ge(outputs, q + 1)
                        nc.vector.tensor_tensor(nodes[0:NP, blocks(q), :], nodes[0:NP, blocks(q), :],
                                                bank[6 + q % 2][0:NP, 0:BATCH * D].rearrange("p (b n) -> p b n", n=D),
                                                ALU.add).then_inc(advanced, 1)
                        if (q + 1) * BATCH % LN_BLOCKS == 0:
                            step = (q + 1) * BATCH // LN_BLOCKS - 1
                            dve.wait_ge(advanced, q + 1)
                            normalize(dve, step, norm)
                            dve.wait_ge(normed, step + 1)
                            b = ln_blocks(step)
                            nc.vector.scalar_tensor_tensor(out=nodes[0:NP, b, :], in0=hidden[0:NP, b, :],
                                                           scalar=one_eps[0:NP, 0:1], in1=nodes[0:NP, b, :],
                                                           op0=ALU.mult, op1=ALU.add)

                @block.sync
                def _(sp):
                    for step in range(LN_STEPS):
                        sp.wait_ge(normed, step + 1)
                        sp.dma_start(hidden_view[:, ln_blocks(step), :],
                                     hidden[0:NP, ln_blocks(step), :]).then_inc(hidden_out, 16)
                    sp.wait_ge(hidden_out, 16 * LN_STEPS)

                @block.gpsimd
                def _(pool):
                    pool.wait_ge(means, BATCHES)
                    nc.gpsimd.memset(sums[0:D, :], 0.0).then_inc(cleared, 1)
                    pool.wait_ge(cleared, 1)

        def finish():
            turned = sem("turned2")
            joined = sem("joined")
            stored = sem("stored")
            with nc.Block() as block:
                @block.tensor
                def _(pe):
                    for q in range(BATCHES):
                        if q >= 8:
                            pe.wait_ge(joined, q - 7)
                        for j in range(BATCH):
                            last = nc.tensor.transpose(bank[q % 8][0:NP, j * D:(j + 1) * D],
                                                       sums[0:D, q * BATCH + j:N:BLOCKS], ident[0:D, 0:D])
                        last.then_inc(turned, 1)

                @block.vector
                def _(dve):
                    for q in range(BATCHES):
                        b = slice(q * BATCH, (q + 1) * BATCH)
                        dve.wait_ge(turned, q + 1)
                        nc.vector.tensor_tensor(nodes[0:NP, b, :], nodes[0:NP, b, :],
                                                bank[q % 8][0:NP, 0:BATCH * D].rearrange("p (b n) -> p b n", n=D),
                                                ALU.add).then_inc(joined, 1)

                @block.sync
                def _(sp):
                    for q in range(BATCHES):
                        b = slice(q * BATCH, (q + 1) * BATCH)
                        sp.wait_ge(joined, q + 1)
                        sp.dma_start(out_view[:, b, :], nodes[0:NP, b, :]).then_inc(stored, 16)
                    sp.wait_ge(stored, 16 * BATCHES)

        prepare()
        sum_near_windows(0)
        sum_far_windows(0)
        update_nodes()
        sum_near_windows(1)
        sum_far_windows(1)
        finish()


def kernel(**inputs):
    import numpy as _np
    import concourse.bacc as _bacc
    from concourse import mybir as _mybir
    from concourse.bass_utils import run_bass_kernel_spmd as _run

    a = {k: _np.ascontiguousarray(v) for k, v in inputs.items()}
    chunks = a["src"].shape[0] // CHUNK
    arrays = {
        "x": a["x"],
        "src_cols": a["src"].reshape(chunks, P, TILES).transpose(1, 0, 2),
        "dst_cols": a["dst"].reshape(chunks, P, TILES).transpose(1, 0, 2),
        "dst_rows": a["dst"].reshape(chunks // SLOTS, SLOTS, CHUNK),
        "edge16": a["edge_attr_16"].reshape(chunks, P, TILES, -1).transpose(0, 3, 2, 1).reshape(chunks, -1, CHUNK),
        "edge32": a["edge_attr_32"].reshape(chunks, P, TILES, -1),
        "w1a": a["L0_gnn_w1a"], "b1a": a["L0_gnn_b1a"], "w1b_t": a["L0_gnn_w1b"].T, "b1b": a["L0_gnn_b1b"],
        "w2a": a["L0_gnn_w2a"], "b2a": a["L0_gnn_b2a"], "w2b": a["L0_gnn_w2b"], "b2b": a["L0_gnn_b2b"],
        "eps": a["L1_gnn_eps"],
    }
    arrays = {k: _np.ascontiguousarray(v) for k, v in arrays.items()}
    nc = _bacc.Bacc("TRN2", target_bir_lowering=False, num_devices=1)
    args = [nc.dram_tensor(f"in_{k}", v.shape, _mybir.dt.from_np(v.dtype), kind="ExternalInput").ap()
            for k, v in arrays.items()]
    out = nc.dram_tensor("out_0", a["x"].shape, F32, kind="ExternalOutput").ap()
    gnn_kernel(nc, *args, out)
    r = _run(nc, [{f"in_{k}": v for k, v in arrays.items()}], core_ids=[0])
    return r.results[0]["out_0"]
```

```python
from contextlib import ExitStack

import concourse.bass as bass
from concourse import mybir

P = 128
WINDOW = 64
WINDOW_BITS = 6
TILES = 5
CHUNK = TILES * P
SLOTS = 5
ROW_PAD = 8
PICK_SLOTS = (2, 4)
PICK_LEAD = 2
LN_EPS = 1e-5

F32 = mybir.dt.float32
I32 = mybir.dt.int32
U32 = mybir.dt.uint32
ALU = mybir.AluOpType
ACT = mybir.ActivationFunctionType
AX = mybir.AxisListType
ENGINES = (mybir.EngineType.Pool, mybir.EngineType.Activation, mybir.EngineType.PE,
           mybir.EngineType.DVE, mybir.EngineType.SP)


def spread(ap, count, axis):
    shape = list(ap.shape)
    shape.insert(axis, count)
    return ap.unsqueeze(axis).broadcast_to(shape)


def gnn_kernel(nc, x, src_cols, src_picks, dst_cols, dst_rows, edge16, edge32, w1a, b1a, w1b_t, b1b,
               w2a, b2a, w2b, b2b, eps, out):
    N, D = x.shape
    D_EDGE = edge16.shape[1]
    CHUNKS = edge16.shape[0]
    H1 = b1a.shape[0]
    H2 = b2a.shape[0]
    NP = 125
    BLOCKS = N // NP
    ITERS = CHUNKS // SLOTS
    SUMS = H1 + 1
    H2C = H2 + 1
    R_PAD = 64
    PSUM_COLS = 512

    LN_BLOCKS = 20
    LN_STEPS = BLOCKS // LN_BLOCKS
    GROUP = P // D
    GROUPS = BLOCKS // GROUP
    ROW_SLOTS = 4
    BATCH = 4
    BATCHES = BLOCKS // BATCH
    PAIRS = BATCH // 2
    AHEAD = 3
    PIECE = 10
    PIECES = BLOCKS // PIECE
    PICKS = len(PICK_SLOTS)
    OUT_BATCH = 10
    OUT_BATCHES = BLOCKS // OUT_BATCH
    assert NP * BLOCKS == N and ITERS * SLOTS == CHUNKS and LN_BLOCKS * LN_STEPS == BLOCKS
    assert GROUP * GROUPS == BLOCKS and BATCH * BATCHES == BLOCKS and LN_BLOCKS % BATCH == 0
    assert 1 << WINDOW_BITS == WINDOW and ITERS <= P and H2C <= R_PAD and BATCH * H2C <= PSUM_COLS
    assert PIECE * PIECES == BLOCKS and PIECE * D <= PSUM_COLS and PICKS == 2
    assert LN_BLOCKS // BATCH >= 3 and PAIRS * NP <= PSUM_COLS and OUT_BATCH * OUT_BATCHES == BLOCKS

    projected_rows = nc.dram_tensor("projected_rows", [N, H1], F32, kind="Internal").ap()
    hidden_rows = nc.dram_tensor("hidden_rows", [N, D], F32, kind="Internal").ap()
    base_rows = nc.dram_tensor("base_rows", [ITERS, ROW_PAD], I32, kind="Internal").ap()
    base_line = nc.dram_tensor("base_line", [ITERS, SLOTS], F32, kind="Internal").ap()
    owner_rows = nc.dram_tensor("owner_rows", [ITERS, PICKS, P], F32, kind="Internal").ap()
    far_rows = nc.dram_tensor("far_rows", [ITERS, ROW_PAD], I32, kind="Internal").ap()

    with ExitStack() as ctx:
        def sb(name, shape, dt=F32):
            return ctx.enter_context(nc.sbuf_tensor(name, shape, dt))

        def sem(name):
            return ctx.enter_context(nc.semaphore(name))

        nodes = sb("nodes", [P, BLOCKS, D])
        hidden = sb("hidden", [P, BLOCKS, D])
        squares = sb("squares", [P, LN_BLOCKS, D])
        stats = sb("stats", [P, 4, BLOCKS])
        self_part = sb("self_part", [P, BLOCKS, H2])
        projected = sb("projected", [P, ROW_SLOTS, GROUP, H1])
        hidden_t = sb("hidden_t", [P, 2, P])
        sums = sb("sums", [P, N + 2 * WINDOW])
        w_msg = sb("w_msg", [P, GROUP, H1])
        w_self = sb("w_self", [P, GROUP, H2])
        w_edge = sb("w_edge", [P, H1])
        w1b_ext_t = sb("w1b_ext_t", [P, SUMS])
        w2a_low = sb("w2a_low", [P, H2])
        w_mean = sb("w_mean", [P, H2C])
        w_out = sb("w_out", [P, 2, D])
        bias_msg = sb("bias_msg", [P, H1])
        bias_self = sb("bias_self", [P, H2])
        eps_col = sb("eps_col", [P, 1])
        one_eps = sb("one_eps", [P, 1])
        ln_eps = sb("ln_eps", [P, 1])
        ident = sb("ident", [P, P])
        window_i = sb("window_i", [P, WINDOW], I32)
        window_f = sb("window_f", [P, WINDOW])
        sources = sb("sources", [P, CHUNKS + SLOTS, TILES], I32)
        destinations = sb("destinations", [P, CHUNKS, TILES], I32)
        offsets = destinations[:, :, :].bitcast(F32)
        by_iter = sb("by_iter", [P, SLOTS, CHUNK], I32)
        low = sb("low", [P, SLOTS])
        high = sb("high", [P, SLOTS])
        low_i = sb("low_i", [P, ROW_PAD], I32)
        far_i = sb("far_i", [P, ROW_PAD], I32)
        far_n = sb("far_n", [P, ROW_PAD], I32)
        base_all = sb("base_all", [P, CHUNKS])
        bases = sb("bases", [1, ITERS * ROW_PAD], I32)
        fars = sb("fars", [1, ITERS * ROW_PAD], I32)
        far_max = sb("far_max", [1, 1])
        far_flag = sb("far_flag", [1, 1], I32)
        index = [sb(f"index{k}", [P, TILES], I32) for k in range(SLOTS)]
        edge_t = [sb(f"edge_t{k}", [D_EDGE, CHUNK]) for k in range(SLOTS)]
        edge_r = [sb(f"edge_r{k}", [P, TILES, D]) for k in range(SLOTS)]
        gathered = [sb(f"gathered{k}", [P, TILES, H1]) for k in range(SLOTS)]
        message = [sb(f"message{k}", [P, TILES, SUMS]) for k in range(SLOTS)]
        onehot = [sb(f"onehot{k}", [P, TILES, WINDOW]) for k in range(SLOTS)]
        pick_source = sb("pick_source", [P, PICKS, P], I32)
        owner = sb("owner", [P, PICKS, P])
        column_quotient_i = sb("column_quotient_i", [P, ITERS, PICKS], I32)
        piece_i = sb("piece_i", [P, PIECES], I32)
        piece_f = sb("piece_f", [P, PIECES])
        owner_in = [sb(f"owner_in{s}", [P, P]) for s in range(PICKS)]
        far_offset = sb("far_offset", [P, TILES])
        inverse = sb("inverse", [P, 2, BATCH])
        update = sb("update", [P, AHEAD, BATCH, R_PAD])
        update_t = sb("update_t", [P, 2, PAIRS, P])

        def carve(whole, first, shape):
            rows, columns = shape
            return whole[:, first:first + rows * columns].rearrange("p (r c) -> p r c", c=columns)

        self_flat = self_part[:, :, :].rearrange("p b n -> p (b n)")
        owner_hot = [carve(self_flat, s * PIECES * P, (PIECES, P)) for s in range(PICKS)]
        placed_rows = [carve(self_flat, (PICKS * PIECES) * P + s * PIECE * D, (PIECE, D)) for s in range(PICKS)]
        place = carve(by_iter[:, :, :].rearrange("p s e -> p (s e)").bitcast(F32), 0, (ITERS * PICKS, PIECE))
        free = [onehot[k][:, :, :].rearrange("p t w -> p (t w)") for k in range(SLOTS)]
        row_quotient_i = carve(free[0].bitcast(I32), 0, (PICKS, P))
        row_remainder, row_carry = (carve(free[k], 0, (PICKS, P)) for k in (1, 2))
        column_remainder, column_carry = (carve(free[k], 0, (ITERS, PICKS)) for k in (3, 4))
        assert PICKS * (PIECES * P + PIECE * D) <= BLOCKS * H2 and PICKS * max(P, ITERS) <= TILES * WINDOW
        assert ITERS * PICKS * PIECE <= SLOTS * CHUNK

        bank = [ctx.enter_context(nc.psum_tensor(f"bank{k}", [P, PSUM_COLS], F32)) for k in range(8)]

        x_view = x.rearrange("(p b) f -> p b f", b=BLOCKS)
        out_view = out.rearrange("(p b) f -> p b f", b=BLOCKS)
        projected_view = projected_rows.rearrange("(p b) f -> p b f", b=BLOCKS)
        hidden_view = hidden_rows.rearrange("(p b) f -> p b f", b=BLOCKS)

        def ln_blocks(step):
            return slice(step * LN_BLOCKS, (step + 1) * LN_BLOCKS)

        def norm_semaphores(layer):
            return {name: sem(f"{name}{layer}") for name in
                    ("totals", "averaged", "centred", "squared", "spreads", "rooted", "inverted", "normed")}

        def centre(dve, step, s):
            b = ln_blocks(step)
            mean, total = stats[0:NP, 0, b], stats[0:NP, 1, b]
            nc.vector.tensor_reduce(total, nodes[0:NP, b, :], AX.X, ALU.add).then_inc(s["totals"], 1)
            dve.wait_ge(s["totals"], step + 1)
            nc.vector.tensor_scalar(mean, total, 1.0 / D, None, ALU.mult).then_inc(s["averaged"], 1)
            dve.wait_ge(s["averaged"], step + 1)
            nc.vector.tensor_tensor(hidden[0:NP, b, :], nodes[0:NP, b, :], spread(mean, D, 2),
                                    ALU.subtract).then_inc(s["centred"], 1)

        def add_squares(dve, step, s):
            dve.wait_ge(s["squared"], step + 1)
            nc.vector.tensor_reduce(stats[0:NP, 1, ln_blocks(step)], squares[0:NP, :, :], AX.X,
                                    ALU.add).then_inc(s["spreads"], 1)

        def scale(dve, step, s):
            b = ln_blocks(step)
            inverse_root = stats[0:NP, 3, b]
            dve.wait_ge(s["rooted"], step + 1)
            nc.vector.reciprocal(inverse_root, stats[0:NP, 2, b]).then_inc(s["inverted"], 1)
            dve.wait_ge(s["inverted"], step + 1)
            nc.vector.scalar_tensor_tensor(out=hidden[0:NP, b, :], in0=hidden[0:NP, b, :], scalar=0.0,
                                           in1=spread(inverse_root, D, 2), op0=ALU.max,
                                           op1=ALU.mult).then_inc(s["normed"], 1)

        def square_and_root(act, step, s):
            b = ln_blocks(step)
            act.wait_ge(s["centred"], step + 1)
            nc.scalar.activation(squares[0:NP, :, :], hidden[0:NP, b, :], ACT.Square).then_inc(s["squared"], 1)
            act.wait_ge(s["spreads"], step + 1)
            nc.scalar.activation(stats[0:NP, 2, b], stats[0:NP, 1, b], ACT.Sqrt, bias=ln_eps[0:NP, 0:1],
                                 scale=1.0 / D).then_inc(s["rooted"], 1)

        def turn_group(pe, g, to, turned, turned_copied):
            if g >= 2:
                pe.wait_ge(turned_copied, g - 1)
            nc.tensor.transpose(bank[to][:, 0:NP],
                                hidden[0:NP, g * GROUP:(g + 1) * GROUP, :].rearrange("p b f -> p (b f)"),
                                ident[0:NP, 0:NP]).then_inc(turned, 1)

        def copy_group(act, g, of, turned, turned_copied, products):
            act.wait_ge(turned, g + 1)
            if g >= 2:
                act.wait_ge(products, g - 1)
            nc.scalar.copy(hidden_t[:, g % 2, 0:NP], bank[of][:, 0:NP]).then_inc(turned_copied, 1)

        def prepare():
            x_in = [sem(f"x_in{step}") for step in range(LN_STEPS)]
            index_in = sem("index_in")
            weights_in = sem("weights_in")
            diagonals_in = sem("diagonals_in")
            diagonals_clear = sem("diagonals_clear")
            ident_clear = sem("ident_clear")
            ident_ready = sem("ident_ready")
            counted = sem("counted")
            fills = sem("fills")
            tail_fills = sem("tail_fills")
            norm = norm_semaphores(0)
            normed = norm["normed"]
            turned = sem("turned")
            turned_copied = sem("turned_copied")
            products = sem("products")
            added_msg = sem("added_msg")
            rows_out = [sem(f"rows_out{k}") for k in range(ROW_SLOTS)]
            w_mean_made = sem("w_mean_made")
            ln_eps_ready = sem("ln_eps_ready")
            N_WEIGHTS = 7
            N_DIAGONALS = 2 * GROUP + 4

            with nc.Block() as block:
                @block.sync
                def _(sp):
                    for step in range(LN_STEPS):
                        sp.dma_start(nodes[0:NP, ln_blocks(step), :], x_view[:, ln_blocks(step), :]
                                     ).then_inc(x_in[step], 16)
                    sp.dma_start(sources[:, 0:CHUNKS, :], src_cols).then_inc(index_in, 16)
                    sp.dma_start(by_iter[0:ITERS, :, :], dst_rows).then_inc(index_in, 16)
                    sp.dma_start(pick_source[0:ITERS, :, :], src_picks).then_inc(index_in, 16)
                    sp.dma_start(destinations[:, :, :], dst_cols).then_inc(index_in, 16)
                    for g in range(GROUPS):
                        sp.wait_ge(added_msg, g + 1)
                        sp.dma_start(projected_view[:, g * GROUP:(g + 1) * GROUP, :],
                                     projected[0:NP, g % ROW_SLOTS, :, :]).then_inc(rows_out[g % ROW_SLOTS], 16)
                    for k in range(ROW_SLOTS):
                        sp.wait_ge(rows_out[k], 16 * ((GROUPS - k + ROW_SLOTS - 1) // ROW_SLOTS))

                @block.scalar
                def _(act):
                    act.dma_start(bias_msg[:, :], b1a.partition_broadcast(P)).then_inc(weights_in, 16)
                    act.dma_start(bias_self[:, :], b2a.partition_broadcast(P)).then_inc(weights_in, 16)
                    act.dma_start(w_edge[0:D_EDGE, :], w1a[D:D + D_EDGE, :]).then_inc(weights_in, 16)
                    act.dma_start(w1b_ext_t[0:H1, 0:H1], w1b_t).then_inc(weights_in, 16)
                    act.dma_start(w1b_ext_t[0:H1, H1:SUMS], b1b.unsqueeze(1)).then_inc(weights_in, 16)
                    act.dma_start(w2a_low[0:H1, :], w2a[D:D + H1, :]).then_inc(weights_in, 16)
                    act.dma_start(eps_col[:, :], eps.partition_broadcast(P)).then_inc(weights_in, 16)
                    act.wait_ge(diagonals_clear, 3)
                    for j in range(GROUP):
                        act.dma_start(w_msg[j * D:(j + 1) * D, j, :], w1a[0:D, :]).then_inc(diagonals_in, 16)
                        act.dma_start(w_self[j * D:(j + 1) * D, j, :], w2a[0:D, :]).then_inc(diagonals_in, 16)
                    for j in range(2):
                        act.dma_start(w_out[j * R_PAD:j * R_PAD + H2, j, :], w2b).then_inc(diagonals_in, 16)
                        act.dma_start(w_out[j * R_PAD + H2:j * R_PAD + H2C, j, :],
                                      b2b.unsqueeze(0)).then_inc(diagonals_in, 16)
                    act.wait_ge(ln_eps_ready, 1)
                    square_and_root(act, 0, norm)
                    for step in range(1, LN_STEPS + 1):
                        for n, g in enumerate(groups_of(step - 1)):
                            if n == 2 and step < LN_STEPS:
                                square_and_root(act, step, norm)
                            copy_group(act, g, g % 2, turned, turned_copied, products)
                    act.wait_ge(weights_in, 16 * N_WEIGHTS)
                    act.wait_ge(diagonals_in, 16 * N_DIAGONALS)

                @block.gpsimd
                def _(pool):
                    nc.gpsimd.memset(w_msg[:, :, :], 0.0).then_inc(diagonals_clear, 1)
                    nc.gpsimd.memset(w_self[:, :, :], 0.0).then_inc(diagonals_clear, 1)
                    nc.gpsimd.memset(w_out[:, :, :], 0.0).then_inc(diagonals_clear, 1)
                    nc.gpsimd.memset(ident[:, :], 0.0).then_inc(ident_clear, 1)
                    pool.wait_ge(ident_clear, 1)
                    nc.gpsimd.affine_select(out=ident[:, :], in_=ident[:, :], compare_op=ALU.not_equal,
                                            fill=1.0, base=0, pattern=[[-1, P]],
                                            channel_multiplier=1).then_inc(ident_ready, 1)
                    nc.gpsimd.iota(window_i[:, :], pattern=[[1, WINDOW]], base=0,
                                   channel_multiplier=0).then_inc(counted, 1)
                    nc.gpsimd.iota(piece_i[:, :], pattern=[[1, PIECES]], base=0,
                                   channel_multiplier=PIECES).then_inc(counted, 1)
                    nc.gpsimd.memset(sources[:, CHUNKS:CHUNKS + SLOTS, :], 0).then_inc(fills, 1)
                    nc.gpsimd.memset(w_mean[:, :], 0.0).then_inc(fills, 1)
                    nc.gpsimd.memset(update[:, :, :, :], 0.0).then_inc(fills, 1)
                    pool.wait_ge(fills, 3)
                    nc.gpsimd.memset(update[:, :, :, H2:H2C], 1.0).then_inc(tail_fills, 1)
                    pool.wait_ge(tail_fills, 1)
                    nc.gpsimd.memset(w_mean[H1:SUMS, H2:H2C], 1.0).then_inc(tail_fills, 1)
                    pool.wait_ge(tail_fills, 2)
                    nc.gpsimd.memset(sums[:, :], 0.0).then_inc(tail_fills, 1)
                    for k in range(SLOTS):
                        nc.gpsimd.memset(message[k][:, :, H1:SUMS], 1.0).then_inc(tail_fills, 1)
                    pool.wait_ge(tail_fills, 3 + SLOTS)

                @block.tensor
                def _(pe):
                    pe.wait_ge(ident_ready, 1)

                    def turn(g):
                        pe.wait_ge(normed, g * GROUP // LN_BLOCKS + 1)
                        turn_group(pe, g, g % 2, turned, turned_copied)

                    turn(0)
                    for g in range(GROUPS):
                        same_step = (g + 1) % (LN_BLOCKS // GROUP) != 0
                        if same_step:
                            turn(g + 1)
                        if g == 0:
                            pe.wait_ge(diagonals_in, 16 * N_DIAGONALS)
                        pe.wait_ge(turned_copied, g + 1)
                        if g >= 2:
                            pe.wait_ge(added_msg, g - 1)
                        nc.tensor.matmul(bank[2 + g % 2][0:NP, 0:GROUP * H1], hidden_t[:, g % 2, 0:NP],
                                         w_msg[:, :, :].rearrange("p j n -> p (j n)"), start=True,
                                         stop=True).then_inc(products, 1)
                        if not same_step and g + 1 < GROUPS:
                            turn(g + 1)
                    pe.wait_ge(weights_in, 16 * N_WEIGHTS)
                    nc.tensor.matmul(bank[6][0:SUMS, 0:H2], w1b_ext_t[0:H1, :], w2a_low[0:H1, :], start=True,
                                     stop=True).then_inc(w_mean_made, 1)

                @block.vector
                def _(dve):
                    def add_bias(g):
                        dve.wait_ge(products, g + 1)
                        if g >= ROW_SLOTS:
                            dve.wait_ge(rows_out[g % ROW_SLOTS], 16 * (g // ROW_SLOTS))
                        nc.vector.tensor_tensor(projected[0:NP, g % ROW_SLOTS, :, :],
                                                bank[2 + g % 2][0:NP, 0:GROUP * H1].rearrange("p (j n) -> p j n", n=H1),
                                                spread(bias_msg[0:NP, :], GROUP, 1), ALU.add).then_inc(added_msg, 1)

                    nc.vector.memset(ln_eps[:, :], LN_EPS).then_inc(ln_eps_ready, 1)
                    dve.wait_ge(x_in[0], 16)
                    centre(dve, 0, norm)
                    add_squares(dve, 0, norm)
                    scale(dve, 0, norm)
                    dve.wait_ge(weights_in, 16 * N_WEIGHTS)
                    for step in range(1, LN_STEPS + 1):
                        for n, g in enumerate(groups_of(step - 1)):
                            if step < LN_STEPS and n == 0:
                                dve.wait_ge(x_in[step], 16)
                                centre(dve, step, norm)
                            if step < LN_STEPS and n == 2:
                                add_squares(dve, step, norm)
                            if step < LN_STEPS and n == 3:
                                scale(dve, step, norm)
                            add_bias(g)
                    dve.wait_ge(counted, 2)
                    nc.vector.tensor_copy(window_f[:, :], window_i[:, :])
                    nc.vector.tensor_copy(piece_f[:, :], piece_i[:, :])
                    nc.vector.tensor_scalar(one_eps[:, :], eps_col[:, :], 1.0, None, ALU.add)
                    dve.wait_ge(index_in, 64)
                    stage_first_round()
                    dve.wait_ge(w_mean_made, 1)
                    dve.wait_ge(fills, 3)
                    nc.vector.tensor_copy(w_mean[0:SUMS, 0:H2], bank[6][0:SUMS, 0:H2])

        def groups_of(step):
            per = LN_BLOCKS // GROUP
            return range(step * per, (step + 1) * per)

        def stage_first_round():
            for k in range(SLOTS):
                nc.vector.tensor_copy(index[k][:, :], sources[:, k, :])

        def gathered_rows(k, row):
            flat = gathered[k][:, :, :].rearrange("p t n -> p (t n)")[:, 0:TILES * row]
            return flat.rearrange("p (t n) -> p t n", n=row)

        def sum_near_windows(layer):
            width, row, table = (SUMS, H1, projected_rows) if layer == 0 else (D, D, hidden_rows)
            index_ready = sem(f"index_ready{layer}")
            edge_in = [sem(f"edge_in{layer}_{k}") for k in range(SLOTS)]
            gather_in = [sem(f"gather_in{layer}_{k}") for k in range(SLOTS)]
            multiplied = sem(f"multiplied{layer}")
            added = sem(f"added{layer}")
            rectified = sem(f"rectified{layer}")
            hot = sem(f"hot{layer}")
            windows = sem(f"windows{layer}")
            summed = sem(f"summed{layer}")
            opened = sem(f"opened{layer}")
            edges_used = multiplied if layer == 0 else added
            picks = {k: s for s, k in enumerate(PICK_SLOTS)} if layer else {}
            if layer:
                owners_in = [sem(f"owners_in{s}") for s in range(PICKS)]
                owners_hot = sem("owners_hot")
                pieces_summed = sem("pieces_summed")
                pieces_placed = sem("pieces_placed")
                picked = sem("picked")
            if layer == 0:
                bound_steps = sem("bound_steps")
                bounds_ready = sem("bounds_ready")
                bounds_out = sem("bounds_out")
                bounds_in = sem("bounds_in")
                farthest = sem("farthest")
                turned = sem("turned_again")
                turned_copied = sem("turned_again_copied")
                products = sem("self_products")
                added_self = sem("added_self")
                offset_ready = sem("offset_ready")

            with nc.Block() as block:
                @block.sync
                def _(sp):
                    if layer:
                        sp.wait_ge(owners_out, 16)
                    with sp.Fori(0, ITERS) as i:
                        for k in range(SLOTS):
                            if k + PICK_LEAD in picks:
                                s = picks[k + PICK_LEAD]
                                sp.wait_ge(owners_hot, PICKS * i + (s + 1))
                                sp.dma_start(owner_in[s][:, :], owner_rows[bass.ds(i, 1), s, :].rearrange(
                                    "o e -> (o e)").partition_broadcast(P)).then_inc(owners_in[s], 16)
                            sp.wait_ge(edges_used, SLOTS * i + (k + 1))
                            if layer == 0:
                                sp.dma_start(edge_t[k][:, :], edge16[bass.ds(SLOTS * i + k, 1), :, :].rearrange(
                                    "o d e -> (o d) e")).then_inc(edge_in[k], 16)
                            else:
                                sp.dma_start(edge_r[k][:, :, :],
                                             edge32[bass.ds(SLOTS * i + k, 1), :, :, :].rearrange(
                                                 "o p t d -> (o p) t d")).then_inc(edge_in[k], 16)

                @block.gpsimd
                def _(pool):
                    with pool.Fori(0, ITERS) as i:
                        for k in range(SLOTS):
                            pool.wait_ge(index_ready, SLOTS * i + (k + 1))
                            pool.wait_ge(rectified, SLOTS * i + (k + 1))
                            pool.sem_inc(opened, 1)
                            for t in range(TILES - (k in picks)):
                                pool.indirect_dma_start(
                                    gathered_rows(k, row)[:, t, :], None, table,
                                    bass.IndirectOffsetOnAxis(ap=index[k][:, t:t + 1], axis=0)
                                ).then_inc(gather_in[k], 16)

                def self_products(pe):
                    turn_group(pe, 0, 4, turned, turned_copied)
                    for g in range(GROUPS):
                        if g + 1 < GROUPS:
                            turn_group(pe, g + 1, 4 + (g + 1) % 2, turned, turned_copied)
                        pe.wait_ge(turned_copied, g + 1)
                        if g >= 2:
                            pe.wait_ge(added_self, g - 1)
                        nc.tensor.matmul(bank[6 + g % 2][0:NP, 0:GROUP * H2], hidden_t[:, g % 2, 0:NP],
                                         w_self[:, :, :].rearrange("p j n -> p (j n)"), start=True,
                                         stop=True).then_inc(products, 1)

                def exchange_bounds(act):
                    act.wait_ge(bounds_ready, 3)
                    act.dma_start(base_line, low[0:ITERS, :]).then_inc(bounds_out, 16)
                    act.dma_start(base_rows, low_i[0:ITERS, :]).then_inc(bounds_out, 16)
                    act.dma_start(far_rows, far_n[0:ITERS, :]).then_inc(bounds_out, 16)
                    act.wait_ge(bounds_out, 48)
                    act.dma_start(base_all[:, :], base_line.rearrange("i s -> (i s)").partition_broadcast(P)
                                  ).then_inc(bounds_in, 16)
                    act.dma_start(bases[:, :], base_rows.rearrange("i s -> (i s)").unsqueeze(0)
                                  ).then_inc(bounds_in, 16)
                    act.dma_start(fars[:, :], far_rows.rearrange("i s -> (i s)").unsqueeze(0)
                                  ).then_inc(bounds_in, 16)

                def find_bounds(dve):
                    nc.vector.memset(low_i[:, :], 0).then_inc(bound_steps, 1)
                    nc.vector.memset(far_n[:, :], 0).then_inc(bound_steps, 1)
                    nc.vector.tensor_reduce(low[0:ITERS, :], by_iter[0:ITERS, :, :], AX.X,
                                            ALU.min).then_inc(bounds_ready, 1)
                    nc.vector.tensor_reduce(high[0:ITERS, :], by_iter[0:ITERS, :, :], AX.X,
                                            ALU.max).then_inc(bound_steps, 1)
                    dve.wait_ge(bounds_ready, 1)
                    dve.wait_ge(bound_steps, 3)
                    nc.vector.tensor_copy(low_i[0:ITERS, 0:SLOTS], low[0:ITERS, :]).then_inc(bounds_ready, 1)
                    nc.vector.tensor_tensor(far_i[0:ITERS, 0:SLOTS], high[0:ITERS, :], low[0:ITERS, :],
                                            ALU.subtract).then_inc(bound_steps, 1)
                    dve.wait_ge(bound_steps, 4)
                    nc.vector.tensor_single_scalar(far_n[0:ITERS, 0:SLOTS], far_i[0:ITERS, 0:SLOTS],
                                                   WINDOW_BITS, ALU.arith_shift_right).then_inc(bounds_ready, 1)

                def add_self_bias(dve):
                    for g in range(GROUPS):
                        dve.wait_ge(products, g + 1)
                        nc.vector.tensor_tensor(self_part[0:NP, g * GROUP:(g + 1) * GROUP, :],
                                                bank[6 + g % 2][0:NP, 0:GROUP * H2].rearrange("p (j n) -> p j n", n=H2),
                                                spread(bias_self[0:NP, :], GROUP, 1), ALU.add).then_inc(added_self, 1)

                def find_offsets(dve):
                    dve.wait_ge(bounds_in, 48)
                    nc.vector.tensor_tensor(offsets, destinations[:, :, :],
                                            spread(base_all[:, :], TILES, 2), ALU.subtract).then_inc(offset_ready, 1)
                    nc.vector.tensor_reduce(far_max[:, :], fars[:, :], AX.X, ALU.max).then_inc(farthest, 1)
                    dve.wait_ge(farthest, 1)
                    nc.vector.tensor_copy(far_flag[:, :], far_max[:, :])
                    dve.wait_ge(offset_ready, 1)

                @block.tensor
                def _(pe):
                    if layer == 0:
                        pe.sem_inc(multiplied, SLOTS)
                    pe.sem_inc(windows, SLOTS)
                    if layer:
                        pe.sem_inc(pieces_summed, PICKS)
                    if layer == 0:
                        self_products(pe)
                    with pe.Fori(0, ITERS) as i:
                        def edge_products(k):
                            pe.wait_ge(edge_in[k], 16 * i + 16)
                            pe.wait_ge(added, SLOTS * i + (k + SLOTS - 1))
                            for t in range(TILES):
                                last = nc.tensor.matmul(bank[k % 3][:, t * H1:(t + 1) * H1],
                                                        edge_t[k][:, t * P:(t + 1) * P],
                                                        w_edge[0:D_EDGE, :], start=True, stop=True)
                            last.then_inc(multiplied, 1)

                        if layer == 0:
                            edge_products(0)
                        for k in range(SLOTS):
                            if k + PICK_LEAD in picks:
                                s = picks[k + PICK_LEAD]
                                pe.wait_ge(owners_hot, PICKS * i + (s + PICKS + 1))
                                pe.wait_ge(pieces_placed, PICKS * i + (s + 1))
                                for j in range(PIECES):
                                    last = nc.tensor.matmul(
                                        bank[6 + s][:, 0:PIECE * D], owner_hot[s][0:NP, j, :],
                                        hidden[0:NP, j * PIECE:(j + 1) * PIECE, :].rearrange("p b f -> p (b f)"),
                                        start=(j == 0), stop=(j == PIECES - 1))
                                last.then_inc(pieces_summed, 1)
                            if layer == 0 and k + 1 < SLOTS:
                                edge_products(k + 1)
                            pe.wait_ge(rectified, SLOTS * i + (k + SLOTS + 1))
                            pe.wait_ge(hot, SLOTS * i + (k + 1))
                            pe.wait_ge(summed, SLOTS * i + (k + 1))
                            for t in range(TILES):
                                last = nc.tensor.matmul(bank[3 + k % 3][0:width, 0:WINDOW],
                                                        message[k][:, t, 0:width], onehot[k][:, t, :],
                                                        start=(t == 0), stop=(t == TILES - 1))
                            last.then_inc(windows, 1)

                @block.scalar
                def _(act):
                    act.sem_inc(rectified, SLOTS)
                    if layer == 0:
                        exchange_bounds(act)
                        for g in range(GROUPS):
                            copy_group(act, g, 4 + g % 2, turned, turned_copied, products)
                    with act.Fori(0, ITERS) as i:
                        for k in range(SLOTS):
                            act.wait_ge(added, SLOTS * i + (k + SLOTS + 1))
                            act.wait_ge(windows, SLOTS * i + (k + 1))
                            nc.scalar.activation(message[k][:, :, 0:row], gathered_rows(k, row),
                                                 ACT.Relu).then_inc(rectified, 1)

                @block.vector
                def _(dve):
                    dve.sem_inc(added, SLOTS)
                    dve.sem_inc(summed, 2)
                    dve.sem_inc(index_ready, SLOTS)
                    if layer:
                        dve.sem_inc(owners_hot, PICKS)
                        dve.sem_inc(pieces_placed, PICKS)
                        dve.sem_inc(picked, PICKS)
                    if layer == 0:
                        find_bounds(dve)
                        add_self_bias(dve)
                        find_offsets(dve)
                    else:
                        nc.vector.scalar_tensor_tensor(out=nodes[0:NP, :, :], in0=hidden[0:NP, :, :],
                                                       scalar=one_eps[0:NP, 0:1], in1=nodes[0:NP, :, :],
                                                       op0=ALU.mult, op1=ALU.add)
                    with dve.Fori(0, ITERS) as i:
                        def add_window(k, base):
                            dve.wait_ge(windows, SLOTS * i + (k + SLOTS + 1))
                            dve.wait_ge(summed, SLOTS * i + (k + 2))
                            nc.vector.tensor_tensor(sums[0:width, bass.ds(base, WINDOW)],
                                                    sums[0:width, bass.ds(base, WINDOW)],
                                                    bank[3 + k % 3][0:width, 0:WINDOW],
                                                    ALU.add).then_inc(summed, 1)

                        def find_owners(s):
                            dve.wait_ge(owners_in[s], 16 * i + 16)
                            dve.wait_ge(pieces_summed, PICKS * i + (s + 1))
                            nc.vector.tensor_tensor(owner_hot[s][0:NP, :, :], spread(owner_in[s][0:NP, :], PIECES, 1),
                                                    spread(piece_f[0:NP, :], P, 2), ALU.is_equal
                                                    ).then_inc(owners_hot, 1)

                        def pick_rows(s, k):
                            dve.wait_ge(pieces_summed, PICKS * i + (s + PICKS + 1))
                            dve.wait_ge(picked, PICKS * i + (s + 1))
                            block_of = place[:, bass.ds(PICKS * i + s, 1), :].rearrange("p o b -> p (o b)")
                            nc.vector.tensor_tensor(placed_rows[s][:, :, :],
                                                    bank[6 + s][:, 0:PIECE * D].rearrange("p (b f) -> p b f", f=D),
                                                    spread(block_of, D, 2), ALU.mult).then_inc(pieces_placed, 1)
                            dve.wait_ge(pieces_placed, PICKS * i + (s + PICKS + 1))
                            dve.wait_ge(rectified, SLOTS * i + (k + 1))
                            nc.vector.tensor_reduce(gathered_rows(k, row)[:, TILES - 1, :],
                                                    placed_rows[s][:, :, :].rearrange("p b f -> p f b"),
                                                    AX.X, ALU.add).then_inc(picked, 1)
                            dve.wait_ge(picked, PICKS * i + (s + PICKS + 1))

                        base_of = []
                        for k in range(SLOTS):
                            if k + PICK_LEAD in picks:
                                find_owners(picks[k + PICK_LEAD])
                            if k in picks:
                                pick_rows(picks[k], k)
                            base_of.append(dve.value_load(bases[0:1, bass.ds(ROW_PAD * i + k, 1)], min_val=0,
                                                          max_val=N - 1))
                            dve.wait_ge(windows, SLOTS * i + (k + 1))
                            nc.vector.tensor_tensor(
                                onehot[k][:, :, :], spread(window_f[:, :], TILES, 1),
                                spread(offsets[:, bass.ds(SLOTS * i + k, 1), :].rearrange("p o t -> p (o t)"),
                                       WINDOW, 2), ALU.is_equal).then_inc(hot, 1)
                            tiles_in = TILES - (k in picks)
                            dve.wait_ge(gather_in[k], 16 * tiles_in * i + 16 * tiles_in)
                            if layer == 0:
                                dve.wait_ge(multiplied, SLOTS * i + (k + SLOTS + 1))
                                other = bank[k % 3][:, 0:TILES * H1].rearrange("p (t n) -> p t n", n=H1)
                            else:
                                dve.wait_ge(edge_in[k], 16 * i + 16)
                                other = edge_r[k][:, :, :]
                            nc.vector.tensor_tensor(gathered_rows(k, row), gathered_rows(k, row), other,
                                                    ALU.add).then_inc(added, 1)
                            nc.vector.tensor_copy(
                                index[k][:, :],
                                sources[:, bass.ds(SLOTS * i + (k + SLOTS), 1), :].rearrange("p o t -> p (o t)")
                            ).then_inc(index_ready, 1)
                            if k:
                                add_window(k - 1, base_of[k - 1])
                        add_window(SLOTS - 1, base_of[SLOTS - 1])

        def sum_far_windows(layer):
            width, row, table = (SUMS, H1, projected_rows) if layer == 0 else (D, D, hidden_rows)
            staged = sem(f"far_staged{layer}")
            edge_in = sem(f"far_edge_in{layer}")
            gather_in = [sem(f"far_gather_in{layer}_{k}") for k in range(SLOTS)]
            multiplied = sem(f"far_multiplied{layer}")
            added = sem(f"far_added{layer}")
            moved = sem(f"far_moved{layer}")
            hot = sem(f"far_hot{layer}")
            window = sem(f"far_window{layer}")

            def clear(*used):
                for s in used:
                    nc.sync.sem_clear(s)
                nc.all_engine_barrier()

            def chunk_messages(i, k):
                chunk = SLOTS * i + k

                with nc.Block() as block:
                    @block.sync
                    def _(sp):
                        if layer == 0:
                            sp.dma_start(edge_t[0][:, :], edge16[bass.ds(chunk, 1), :, :].rearrange(
                                "o d e -> (o d) e")).then_inc(edge_in, 16)
                        else:
                            sp.dma_start(edge_r[0][:, :, :], edge32[bass.ds(chunk, 1), :, :, :].rearrange(
                                "o p t d -> (o p) t d")).then_inc(edge_in, 16)

                    @block.gpsimd
                    def _(pool):
                        pool.wait_ge(staged, 1)
                        for t in range(TILES):
                            pool.indirect_dma_start(
                                gathered_rows(0, row)[:, t, :], None, table,
                                bass.IndirectOffsetOnAxis(ap=index[0][:, t:t + 1], axis=0)
                            ).then_inc(gather_in[k], 16)

                    @block.tensor
                    def _(pe):
                        if layer == 0:
                            pe.wait_ge(edge_in, 16)
                            for t in range(TILES):
                                last = nc.tensor.matmul(bank[0][:, t * H1:(t + 1) * H1],
                                                        edge_t[0][:, t * P:(t + 1) * P], w_edge[0:D_EDGE, :],
                                                        start=True, stop=True)
                            last.then_inc(multiplied, 1)

                    @block.scalar
                    def _(act):
                        act.wait_ge(added, 1)
                        nc.scalar.activation(message[0][:, :, 0:row], gathered_rows(0, row), ACT.Relu)

                    @block.vector
                    def _(dve):
                        nc.vector.tensor_copy(index[0][:, :], sources[:, bass.ds(chunk, 1), :].rearrange(
                            "p o t -> p (o t)")).then_inc(staged, 1)
                        nc.vector.tensor_copy(far_offset[:, :], offsets[:, bass.ds(chunk, 1), :].rearrange(
                            "p o t -> p (o t)"))
                        dve.wait_ge(gather_in[k], 16 * TILES * i + 16 * TILES)
                        if layer == 0:
                            dve.wait_ge(multiplied, 1)
                            other = bank[0][:, 0:TILES * H1].rearrange("p (t n) -> p t n", n=H1)
                        else:
                            dve.wait_ge(edge_in, 16)
                            other = edge_r[0][:, :, :]
                        nc.vector.tensor_tensor(gathered_rows(0, row), gathered_rows(0, row), other,
                                                ALU.add).then_inc(added, 1)
                clear(staged, edge_in, multiplied, added)

            def add_window(base, w):
                with nc.Block() as block:
                    @block.vector
                    def _(dve):
                        nc.vector.tensor_scalar(far_offset[:, :], far_offset[:, :], float(-WINDOW), None,
                                                ALU.add).then_inc(moved, 1)
                        dve.wait_ge(moved, 1)
                        nc.vector.tensor_tensor(onehot[0][:, :, :], spread(window_f[:, :], TILES, 1),
                                                spread(far_offset[:, :], WINDOW, 2), ALU.is_equal).then_inc(hot, 1)
                        dve.wait_ge(window, 1)
                        first = nc.s_assert_within(base + w * WINDOW, 0, N - 1 + WINDOW)
                        nc.vector.tensor_tensor(sums[0:width, bass.ds(first, WINDOW)],
                                                sums[0:width, bass.ds(first, WINDOW)],
                                                bank[3][0:width, 0:WINDOW], ALU.add)

                    @block.tensor
                    def _(pe):
                        pe.wait_ge(hot, 1)
                        for t in range(TILES):
                            last = nc.tensor.matmul(bank[3][0:width, 0:WINDOW], message[0][:, t, 0:width],
                                                    onehot[0][:, t, :], start=(t == 0), stop=(t == TILES - 1))
                        last.then_inc(window, 1)
                clear(moved, hot, window)

            some = nc.values_load(far_flag[0:1, 0:1], min_val=0, max_val=N)
            with nc.If(some > 0):
                with nc.Fori(0, ITERS) as i:
                    for k in range(SLOTS):
                        chunk_messages(i, k)
                        base = nc.values_load(bases[0:1, bass.ds(ROW_PAD * i + k, 1)], min_val=0, max_val=N - 1)
                        last = nc.values_load(fars[0:1, bass.ds(ROW_PAD * i + k, 1)], min_val=0,
                                              max_val=(N - 1) // WINDOW)
                        with nc.Fori(1, last + 1) as w:
                            add_window(base, w)

        def divide_sources(dve, stages, source, quotient_i, remainder, carry):
            nc.vector.tensor_scalar(quotient_i, source, 1.0 / PIECE, 0.5 / PIECE - 0.5, ALU.mult,
                                    ALU.add).then_inc(stages, 1)
            dve.wait_ge(stages, 1)
            nc.vector.scalar_tensor_tensor(out=remainder, in0=quotient_i, scalar=float(-PIECE), in1=source,
                                           op0=ALU.mult, op1=ALU.add).then_inc(stages, 1)
            dve.wait_ge(stages, 2)
            nc.vector.tensor_scalar(carry, remainder, float(PIECE), None, ALU.is_ge).then_inc(stages, 1)
            dve.wait_ge(stages, 3)

        owners_out = sem("owners_out")

        def update_nodes():
            row_division = sem("row_division")
            column_division = sem("column_division")
            owners_ready = sem("owners_ready")
            norm = norm_semaphores(1)
            normed = norm["normed"]
            means = sem("means")
            capped = sem("capped")
            inverted = sem("inverted_counts")
            scaled = sem("scaled")
            shifted = sem("shifted")
            updates = sem("updates")
            turned = sem("turned1")
            turned_copied = sem("turned_copied1")
            outputs = sem("outputs")
            advanced = sem("advanced")
            hidden_out = sem("hidden_out")
            cleared = sem("cleared")
            PER_STEP = LN_BLOCKS // BATCH
            TURN, OUTPUT = AHEAD, AHEAD + 2

            def blocks(q):
                return slice(q * BATCH, (q + 1) * BATCH)

            with nc.Block() as block:
                @block.tensor
                def _(pe):
                    def mean(q):
                        if q >= AHEAD:
                            pe.wait_ge(scaled, q - AHEAD + 1)
                        for j in range(BATCH):
                            last = nc.tensor.matmul(bank[q % AHEAD][0:NP, j * H2C:(j + 1) * H2C],
                                                    sums[0:SUMS, q * BATCH + j:N:BLOCKS], w_mean[0:SUMS, :],
                                                    start=True, stop=True)
                        last.then_inc(means, 1)

                    def turn(q):
                        pe.wait_ge(updates, q + 1)
                        if q >= 2:
                            pe.wait_ge(turned_copied, q - 1)
                        for j in range(PAIRS):
                            last = nc.tensor.transpose(
                                bank[TURN + q % 2][:, j * NP:(j + 1) * NP],
                                update[0:NP, q % AHEAD, 2 * j:2 * j + 2, :].rearrange("p b f -> p (b f)"),
                                ident[0:NP, 0:NP])
                        last.then_inc(turned, 1)

                    for q in range(AHEAD):
                        mean(q)
                    turn(0)
                    for q in range(BATCHES):
                        if q + 1 < BATCHES:
                            turn(q + 1)
                        pe.wait_ge(turned_copied, q + 1)
                        if q >= 2:
                            pe.wait_ge(advanced, q - 1)
                        for j in range(PAIRS):
                            last = nc.tensor.matmul(bank[OUTPUT + q % 2][0:NP, j * 2 * D:(j + 1) * 2 * D],
                                                    update_t[:, q % 2, j, 0:NP],
                                                    w_out[:, :, :].rearrange("p j n -> p (j n)"),
                                                    start=True, stop=True)
                        last.then_inc(outputs, 1)
                        if q + AHEAD < BATCHES:
                            mean(q + AHEAD)

                @block.scalar
                def _(act):
                    def rectify(q):
                        act.wait_ge(shifted, q + 1)
                        nc.scalar.activation(update[0:NP, q % AHEAD, :, 0:H2], update[0:NP, q % AHEAD, :, 0:H2],
                                             ACT.Relu).then_inc(updates, 1)

                    rectify(0)
                    for q in range(BATCHES):
                        if q + 1 < BATCHES:
                            rectify(q + 1)
                        act.wait_ge(turned, q + 1)
                        if q >= 2:
                            act.wait_ge(outputs, q - 1)
                        nc.scalar.copy(update_t[:, q % 2, :, 0:NP],
                                       bank[TURN + q % 2][:, 0:PAIRS * NP].rearrange("p (j n) -> p j n", n=NP)
                                       ).then_inc(turned_copied, 1)
                        if q % PER_STEP == 1 and q > 1:
                            square_and_root(act, q // PER_STEP - 1, norm)
                    square_and_root(act, LN_STEPS - 1, norm)
                    act.wait_ge(owners_ready, 1)
                    act.dma_start(owner_rows, owner[0:ITERS, :, :]).then_inc(owners_out, 16)

                @block.vector
                def _(dve):
                    def first_layer(q):
                        s = q % AHEAD
                        dve.wait_ge(means, q + 1)
                        view = bank[s][0:NP, 0:BATCH * H2C].rearrange("p (b n) -> p b n", n=H2C)
                        count = view[:, :, H2:H2C].rearrange("p b o -> p (b o)")
                        nc.vector.tensor_scalar(inverse[0:NP, 0, :], count, 1.0, None, ALU.max).then_inc(capped, 1)
                        dve.wait_ge(capped, q + 1)
                        nc.vector.reciprocal(inverse[0:NP, 1, :], inverse[0:NP, 0, :]).then_inc(inverted, 1)
                        dve.wait_ge(inverted, q + 1)
                        if q >= AHEAD:
                            dve.wait_ge(turned, q - AHEAD + 1)
                        nc.vector.tensor_tensor(update[0:NP, s, :, 0:H2], view[:, :, 0:H2],
                                                spread(inverse[0:NP, 1, :], H2, 2), ALU.mult).then_inc(scaled, 1)
                        dve.wait_ge(scaled, q + 1)
                        nc.vector.tensor_tensor(update[0:NP, s, :, 0:H2], update[0:NP, s, :, 0:H2],
                                                self_part[0:NP, blocks(q), :], ALU.add).then_inc(shifted, 1)

                    stage_first_round()
                    first_layer(0)
                    first_layer(1)
                    for q in range(BATCHES):
                        if q + 2 < BATCHES:
                            first_layer(q + 2)
                        dve.wait_ge(outputs, q + 1)
                        nc.vector.tensor_tensor(nodes[0:NP, blocks(q), :], nodes[0:NP, blocks(q), :],
                                                bank[OUTPUT + q % 2][0:NP, 0:BATCH * D].rearrange(
                                                    "p (b n) -> p b n", n=D), ALU.add).then_inc(advanced, 1)
                        step = q // PER_STEP - 1
                        if step >= 0 and q % PER_STEP == 1:
                            add_squares(dve, step, norm)
                        if step >= 0 and q % PER_STEP == 2:
                            scale(dve, step, norm)
                        if q % PER_STEP == PER_STEP - 1:
                            dve.wait_ge(advanced, q + 1)
                            centre(dve, q // PER_STEP, norm)
                    add_squares(dve, LN_STEPS - 1, norm)
                    scale(dve, LN_STEPS - 1, norm)
                    divide_sources(dve, row_division, pick_source[0:ITERS, :, :], row_quotient_i[0:ITERS, :, :],
                                   row_remainder[0:ITERS, :, :], row_carry[0:ITERS, :, :])
                    nc.vector.tensor_tensor(owner[0:ITERS, :, :], row_quotient_i[0:ITERS, :, :],
                                            row_carry[0:ITERS, :, :], ALU.add).then_inc(owners_ready, 1)
                    columns = sources[:, 0:CHUNKS, TILES - 1:TILES].rearrange("p (i k) o -> p i (k o)", k=SLOTS)
                    columns = columns[:, :, PICK_SLOTS[0]:SLOTS:PICK_LEAD]
                    divide_sources(dve, column_division, columns, column_quotient_i[:, :, :],
                                   column_remainder[:, :, :], column_carry[:, :, :])
                    nc.vector.scalar_tensor_tensor(out=column_remainder[:, :, :], in0=column_carry[:, :, :],
                                                   scalar=float(-PIECE), in1=column_remainder[:, :, :],
                                                   op0=ALU.mult, op1=ALU.add).then_inc(column_division, 1)
                    dve.wait_ge(column_division, 4)
                    nc.vector.tensor_tensor(
                        place[:, :, :],
                        spread(window_f[:, 0:PIECE], ITERS * PICKS, 1),
                        spread(column_remainder[:, :, :].rearrange("p i s -> p (i s)"), PIECE, 2),
                        ALU.is_equal)

                @block.sync
                def _(sp):
                    for step in range(LN_STEPS):
                        sp.wait_ge(normed, step + 1)
                        sp.dma_start(hidden_view[:, ln_blocks(step), :],
                                     hidden[0:NP, ln_blocks(step), :]).then_inc(hidden_out, 16)
                    sp.wait_ge(hidden_out, 16 * LN_STEPS)

                @block.gpsimd
                def _(pool):
                    pool.wait_ge(means, BATCHES)
                    nc.gpsimd.memset(sums[0:D, :], 0.0).then_inc(cleared, 1)
                    pool.wait_ge(cleared, 1)

        def finish():
            turned = sem("turned2")
            joined = sem("joined")
            stored = sem("stored")
            with nc.Block() as block:
                @block.tensor
                def _(pe):
                    for q in range(OUT_BATCHES):
                        if q >= 8:
                            pe.wait_ge(joined, q - 7)
                        for j in range(OUT_BATCH):
                            last = nc.tensor.transpose(bank[q % 8][0:NP, j * D:(j + 1) * D],
                                                       sums[0:D, q * OUT_BATCH + j:N:BLOCKS], ident[0:D, 0:D])
                        last.then_inc(turned, 1)

                @block.vector
                def _(dve):
                    for q in range(OUT_BATCHES):
                        b = slice(q * OUT_BATCH, (q + 1) * OUT_BATCH)
                        dve.wait_ge(turned, q + 1)
                        nc.vector.tensor_tensor(nodes[0:NP, b, :], nodes[0:NP, b, :],
                                                bank[q % 8][0:NP, 0:OUT_BATCH * D].rearrange("p (b n) -> p b n", n=D),
                                                ALU.add).then_inc(joined, 1)

                @block.sync
                def _(sp):
                    for q in range(OUT_BATCHES):
                        b = slice(q * OUT_BATCH, (q + 1) * OUT_BATCH)
                        sp.wait_ge(joined, q + 1)
                        sp.dma_start(out_view[:, b, :], nodes[0:NP, b, :]).then_inc(stored, 16)
                    sp.wait_ge(stored, 16 * OUT_BATCHES)

        prepare()
        sum_near_windows(0)
        sum_far_windows(0)
        update_nodes()
        sum_near_windows(1)
        sum_far_windows(1)
        finish()


def kernel(**inputs):
    import numpy as _np
    import concourse.bacc as _bacc
    from concourse import mybir as _mybir
    from concourse.bass_utils import run_bass_kernel_spmd as _run

    a = {k: _np.ascontiguousarray(v) for k, v in inputs.items()}
    chunks = a["src"].shape[0] // CHUNK
    arrays = {
        "x": a["x"],
        "src_cols": a["src"].reshape(chunks, P, TILES).transpose(1, 0, 2),
        "src_picks": a["src"].reshape(chunks // SLOTS, SLOTS, P, TILES)[..., TILES - 1][:, list(PICK_SLOTS)],
        "dst_cols": a["dst"].reshape(chunks, P, TILES).transpose(1, 0, 2),
        "dst_rows": a["dst"].reshape(chunks // SLOTS, SLOTS, CHUNK),
        "edge16": a["edge_attr_16"].reshape(chunks, P, TILES, -1).transpose(0, 3, 2, 1).reshape(chunks, -1, CHUNK),
        "edge32": a["edge_attr_32"].reshape(chunks, P, TILES, -1),
        "w1a": a["L0_gnn_w1a"], "b1a": a["L0_gnn_b1a"], "w1b_t": a["L0_gnn_w1b"].T, "b1b": a["L0_gnn_b1b"],
        "w2a": a["L0_gnn_w2a"], "b2a": a["L0_gnn_b2a"], "w2b": a["L0_gnn_w2b"], "b2b": a["L0_gnn_b2b"],
        "eps": a["L1_gnn_eps"],
    }
    arrays = {k: _np.ascontiguousarray(v) for k, v in arrays.items()}
    nc = _bacc.Bacc("TRN2", target_bir_lowering=False, num_devices=1)
    args = [nc.dram_tensor(f"in_{k}", v.shape, _mybir.dt.from_np(v.dtype), kind="ExternalInput").ap()
            for k, v in arrays.items()]
    out = nc.dram_tensor("out_0", a["x"].shape, F32, kind="ExternalOutput").ap()
    gnn_kernel(nc, *args, out)
    r = _run(nc, [{f"in_{k}": v for k, v in arrays.items()}], core_ids=[0])
    return r.results[0]["out_0"]
```

```python
from collections import namedtuple
from contextlib import ExitStack

import concourse.bass as bass
from concourse import mybir

P = 128
WINDOW = 64
WINDOW_BITS = 6
TILES = 5
CHUNK = TILES * P
SLOTS = 5
ROW_PAD = 8
PIECE_BITS = 4
PICK_SLOTS = (1, 2, 3, 4)
LN_EPS = 1e-5

F32 = mybir.dt.float32
BF16 = mybir.dt.bfloat16
I32 = mybir.dt.int32
ALU = mybir.AluOpType
ACT = mybir.ActivationFunctionType
AX = mybir.AxisListType

Pick = namedtuple("Pick", "slot early find sum pick")
LAYER_PICKS = ((Pick(3, 1, 4, 4, 2), Pick(4, 0, 1, 1, 3)),
               (Pick(1, 1, 3, 3, 1), Pick(2, 1, 4, 4, 2), Pick(3, 0, 0, 0, 3), Pick(4, 0, 1, 1, 4)))


def spread(ap, count, axis):
    shape = list(ap.shape)
    shape.insert(axis, count)
    return ap.unsqueeze(axis).broadcast_to(shape)


def gnn_kernel(nc, x, src_cols, src_picks, dst_cols, dst_rows, edge16, edge32, w1a, b1a, w1b_t, b1b,
               w2a, b2a, w2b, b2b, eps, out):
    N, D = x.shape
    EDGE_ROWS = edge16.shape[1]
    D_EDGE = EDGE_ROWS // TILES
    PICK_ROW = P - D
    CHUNKS = edge16.shape[0]
    H1 = b1a.shape[0]
    H2 = b2a.shape[0]
    NP = 125
    BLOCKS = N // NP
    ITERS = CHUNKS // SLOTS
    SUMS = H1 + 1
    H2C = H2 + 1
    R_PAD = 64
    PSUM_COLS = 512

    LN_BLOCKS = 20
    LN_STEPS = BLOCKS // LN_BLOCKS
    GROUP = P // D
    GROUPS = BLOCKS // GROUP
    ROW_SLOTS = 4
    BATCH = 4
    BATCHES = BLOCKS // BATCH
    PAIRS = BATCH // 2
    AHEAD = 3
    PIECE = 1 << PIECE_BITS
    PIECES = -(-BLOCKS // PIECE)
    PARTS = 3
    PICKS = len(PICK_SLOTS)
    OUT_BATCH = 10
    OUT_BATCHES = BLOCKS // OUT_BATCH
    assert NP * BLOCKS == N and ITERS * SLOTS == CHUNKS and LN_BLOCKS * LN_STEPS == BLOCKS
    assert GROUP * GROUPS == BLOCKS and BATCH * BATCHES == BLOCKS and LN_BLOCKS % BATCH == 0
    assert 1 << WINDOW_BITS == WINDOW and ITERS < P and H2C <= R_PAD and BATCH * H2C <= PSUM_COLS
    assert PIECES >= 3 and PIECE <= WINDOW and PIECE * D <= PSUM_COLS and EDGE_ROWS < PICK_ROW
    assert LN_BLOCKS // GROUP == SLOTS and LN_STEPS >= 3
    assert LN_BLOCKS // BATCH >= 3 and PAIRS * NP <= PSUM_COLS and OUT_BATCH * OUT_BATCHES == BLOCKS

    projected_rows = nc.dram_tensor("projected_rows", [N, H1], F32, kind="Internal").ap()
    hidden_rows = nc.dram_tensor("hidden_rows", [N, D], F32, kind="Internal").ap()
    base_rows = nc.dram_tensor("base_rows", [ITERS, ROW_PAD], I32, kind="Internal").ap()
    base_line = nc.dram_tensor("base_line", [ITERS, SLOTS], F32, kind="Internal").ap()
    owner_rows = nc.dram_tensor("owner_rows", [ITERS + 1, PICKS, P], F32, kind="Internal").ap()
    far_rows = nc.dram_tensor("far_rows", [ITERS, ROW_PAD], I32, kind="Internal").ap()

    with ExitStack() as ctx:
        def sb(name, shape, dt=F32):
            return ctx.enter_context(nc.sbuf_tensor(name, shape, dt))

        def sem(name):
            return ctx.enter_context(nc.semaphore(name))

        nodes = sb("nodes", [P, BLOCKS, D])
        hidden = sb("hidden", [P, BLOCKS, D])
        squares = sb("squares", [P, LN_BLOCKS, D])
        stats = sb("stats", [P, 4, BLOCKS])
        self_part = sb("self_part", [P, BLOCKS, H2])
        projected = sb("projected", [P, ROW_SLOTS, GROUP, H1])
        hidden_t = sb("hidden_t", [P, 2, P])
        sums = sb("sums", [P, N + 2 * WINDOW])
        w_msg = sb("w_msg", [P, GROUP, H1])
        w_self = sb("w_self", [P, GROUP, H2])
        w_edge = sb("w_edge", [P, TILES, H1])
        w1b_ext_t = sb("w1b_ext_t", [P, SUMS])
        w2a_low = sb("w2a_low", [P, H2])
        w_mean = sb("w_mean", [P, H2C])
        w_out = sb("w_out", [P, 2, D])
        bias_msg = sb("bias_msg", [P, H1])
        bias_self = sb("bias_self", [P, H2])
        eps_col = sb("eps_col", [P, 1])
        one_eps = sb("one_eps", [P, 1])
        ln_eps = sb("ln_eps", [P, 1])
        ident = sb("ident", [P, P])
        window_i = sb("window_i", [P, WINDOW], I32)
        window_f = sb("window_f", [P, WINDOW])
        sources = sb("sources", [P, CHUNKS + SLOTS, TILES], I32)
        destinations = sb("destinations", [P, CHUNKS, TILES], I32)
        offsets = destinations[:, :, :].bitcast(F32)
        by_iter = sb("by_iter", [P, SLOTS, CHUNK], I32)
        low = sb("low", [P, SLOTS])
        high = sb("high", [P, SLOTS])
        low_i = sb("low_i", [P, ROW_PAD], I32)
        far_i = sb("far_i", [P, ROW_PAD], I32)
        far_n = sb("far_n", [P, ROW_PAD], I32)
        base_all = sb("base_all", [P, CHUNKS])
        bases = sb("bases", [1, ITERS * ROW_PAD], I32)
        fars = sb("fars", [1, ITERS * ROW_PAD], I32)
        far_max = sb("far_max", [1, 1])
        far_flag = sb("far_flag", [1, 1], I32)
        index = [sb(f"index{k}", [P, TILES], I32) for k in range(SLOTS)]
        edge_r = [sb(f"edge_r{k}", [P, TILES, D]) for k in range(SLOTS)]
        edge_t = [edge_r[k][:, :, :].rearrange("p t d -> p (t d)")[:, 0:P] for k in range(SLOTS)]
        gathered = [sb(f"gathered{k}", [P, TILES, H1]) for k in range(SLOTS)]
        message = [sb(f"message{k}", [P, TILES, SUMS]) for k in range(SLOTS)]
        onehot = [sb(f"onehot{k}", [P, TILES, WINDOW]) for k in range(SLOTS)]
        pick_source = sb("pick_source", [P, PICKS, P], I32)
        piece_i = sb("piece_i", [P, PIECES], I32)
        piece_f = sb("piece_f", [P, PIECES])
        far_offset = sb("far_offset", [P, TILES])
        inverse = sb("inverse", [P, 2, BATCH])
        update = sb("update", [P, AHEAD, BATCH, R_PAD])

        owner_hot_halves = sb("owner_hot_halves", [P, PICKS, PIECES, P], BF16)
        place_hot = [sb(f"place_hot{s}", [P, PIECE]) for s in range(PICKS)]
        wide_rows = sb("wide_rows", [P, P])

        assert PARTS * D <= 2 * H2
        hidden_parts = self_part[:, :, :].rearrange("p b n -> p (b n)").bitcast(BF16)[
            :, 0:PARTS * BLOCKS * D].rearrange("p (t b f) -> p t b f", b=BLOCKS, f=D)

        projected_flat = projected[:, :, :, :].rearrange("p s j n -> p (s j n)")
        update_t = projected_flat[:, 0:2 * PAIRS * P].rearrange("p (s j n) -> p s j n", j=PAIRS, n=P)
        rest = projected_flat[:, 2 * PAIRS * P:]
        placed_rows = rest[:, 0:PIECE * D].rearrange("p (b f) -> p b f", f=D)
        owner_in = [rest[:, PIECE * D + s * P:PIECE * D + (s + 1) * P] for s in range(PICKS)]
        assert 2 * PAIRS * P + PIECE * D + PICKS * P <= ROW_SLOTS * GROUP * H1

        by_iter_flat = by_iter[:, :, :].rearrange("p s e -> p (s e)")

        def carve(n, shape):
            rows, columns = shape
            first = n * PICKS * P
            assert rows * columns <= PICKS * P and first + PICKS * P <= SLOTS * CHUNK
            return by_iter_flat[:, first:first + rows * columns].rearrange("p (r c) -> p r c", c=columns)

        row_whole, row_block = carve(0, (PICKS, P)), carve(1, (PICKS, P))
        owner = row_whole.bitcast(F32)
        row_rest, row_carry = (carve(n, (PICKS, P)).bitcast(F32) for n in (2, 3))
        column_rest, column_carry = (carve(n, (ITERS + 1, PICKS)).bitcast(F32) for n in (2, 3))
        column_block, column_whole = carve(1, (ITERS + 1, PICKS)), carve(4, (ITERS + 1, PICKS))
        block_in_piece = column_whole

        bank = [ctx.enter_context(nc.psum_tensor(f"bank{k}", [P, PSUM_COLS], F32)) for k in range(8)]

        x_view = x.rearrange("(p b) f -> p b f", b=BLOCKS)
        out_view = out.rearrange("(p b) f -> p b f", b=BLOCKS)
        projected_view = projected_rows.rearrange("(p b) f -> p b f", b=BLOCKS)
        hidden_view = hidden_rows.rearrange("(p b) f -> p b f", b=BLOCKS)

        def ln_blocks(step):
            return slice(step * LN_BLOCKS, (step + 1) * LN_BLOCKS)

        def norm_semaphores(layer):
            return {name: sem(f"{name}{layer}") for name in
                    ("totals", "averaged", "centred", "squared", "spreads", "rooted", "inverted", "normed")}

        def centre(dve, step, s):
            b = ln_blocks(step)
            mean, total = stats[0:NP, 0, b], stats[0:NP, 1, b]
            nc.vector.tensor_reduce(total, nodes[0:NP, b, :], AX.X, ALU.add).then_inc(s["totals"], 1)
            dve.wait_ge(s["totals"], step + 1)
            nc.vector.tensor_scalar(mean, total, 1.0 / D, None, ALU.mult).then_inc(s["averaged"], 1)
            dve.wait_ge(s["averaged"], step + 1)
            nc.vector.tensor_tensor(hidden[0:NP, b, :], nodes[0:NP, b, :], spread(mean, D, 2),
                                    ALU.subtract).then_inc(s["centred"], 1)

        def add_squares(dve, step, s):
            dve.wait_ge(s["squared"], step + 1)
            nc.vector.tensor_reduce(stats[0:NP, 1, ln_blocks(step)], squares[0:NP, :, :], AX.X,
                                    ALU.add).then_inc(s["spreads"], 1)

        def scale(dve, step, s):
            b = ln_blocks(step)
            inverse_root = stats[0:NP, 3, b]
            dve.wait_ge(s["rooted"], step + 1)
            nc.vector.reciprocal(inverse_root, stats[0:NP, 2, b]).then_inc(s["inverted"], 1)
            dve.wait_ge(s["inverted"], step + 1)
            nc.vector.scalar_tensor_tensor(out=hidden[0:NP, b, :], in0=hidden[0:NP, b, :], scalar=0.0,
                                           in1=spread(inverse_root, D, 2), op0=ALU.max,
                                           op1=ALU.mult).then_inc(s["normed"], 1)

        def square_and_root(act, step, s):
            b = ln_blocks(step)
            act.wait_ge(s["centred"], step + 1)
            nc.scalar.activation(squares[0:NP, :, :], hidden[0:NP, b, :], ACT.Square).then_inc(s["squared"], 1)
            act.wait_ge(s["spreads"], step + 1)
            nc.scalar.activation(stats[0:NP, 2, b], stats[0:NP, 1, b], ACT.Sqrt, bias=ln_eps[0:NP, 0:1],
                                 scale=1.0 / D).then_inc(s["rooted"], 1)

        def turn_group(pe, g, to, turned, turned_copied):
            if g >= 2:
                pe.wait_ge(turned_copied, g - 1)
            nc.tensor.transpose(bank[to][:, 0:NP],
                                hidden[0:NP, g * GROUP:(g + 1) * GROUP, :].rearrange("p b f -> p (b f)"),
                                ident[0:NP, 0:NP]).then_inc(turned, 1)

        def copy_group(act, g, of, turned, turned_copied, products):
            act.wait_ge(turned, g + 1)
            if g >= 2:
                act.wait_ge(products, g - 1)
            nc.scalar.copy(hidden_t[:, g % 2, 0:NP], bank[of][:, 0:NP]).then_inc(turned_copied, 1)

        def prepare():
            x_in = [sem(f"x_in{step}") for step in range(LN_STEPS)]
            index_in = sem("index_in")
            weights_in = sem("weights_in")
            diagonals_in = sem("diagonals_in")
            diagonals_clear = sem("diagonals_clear")
            ident_clear = sem("ident_clear")
            ident_ready = sem("ident_ready")
            counted = sem("counted")
            fills = sem("fills")
            tail_fills = sem("tail_fills")
            norm = norm_semaphores(0)
            normed = norm["normed"]
            turned = sem("turned")
            turned_copied = sem("turned_copied")
            products = sem("products")
            added_msg = sem("added_msg")
            rows_out = [sem(f"rows_out{k}") for k in range(ROW_SLOTS)]
            w_mean_made = sem("w_mean_made")
            ln_eps_ready = sem("ln_eps_ready")
            N_WEIGHTS = 6
            N_DIAGONALS = 2 * GROUP + 4 + TILES + 2

            with nc.Block() as block:
                @block.sync
                def _(sp):
                    for step in range(LN_STEPS):
                        sp.dma_start(nodes[0:NP, ln_blocks(step), :], x_view[:, ln_blocks(step), :]
                                     ).then_inc(x_in[step], 16)
                    sp.dma_start(sources[:, 0:CHUNKS, :], src_cols).then_inc(index_in, 16)
                    sp.dma_start(by_iter[0:ITERS, :, :], dst_rows).then_inc(index_in, 16)
                    sp.dma_start(pick_source[0:ITERS, :, :], src_picks).then_inc(index_in, 16)
                    sp.dma_start(pick_source[ITERS:ITERS + 1, :, :], src_picks[0:1, :, :]).then_inc(index_in, 16)
                    sp.dma_start(destinations[:, :, :], dst_cols).then_inc(index_in, 16)
                    for g in range(GROUPS):
                        sp.wait_ge(added_msg, g + 1)
                        sp.dma_start(projected_view[:, g * GROUP:(g + 1) * GROUP, :],
                                     projected[0:NP, g % ROW_SLOTS, :, :]).then_inc(rows_out[g % ROW_SLOTS], 16)
                    for k in range(ROW_SLOTS):
                        sp.wait_ge(rows_out[k], 16 * ((GROUPS - k + ROW_SLOTS - 1) // ROW_SLOTS))

                @block.scalar
                def _(act):
                    act.dma_start(bias_msg[:, :], b1a.partition_broadcast(P)).then_inc(weights_in, 16)
                    act.dma_start(bias_self[:, :], b2a.partition_broadcast(P)).then_inc(weights_in, 16)
                    act.dma_start(w1b_ext_t[0:H1, 0:H1], w1b_t).then_inc(weights_in, 16)
                    act.dma_start(w1b_ext_t[0:H1, H1:SUMS], b1b.unsqueeze(1)).then_inc(weights_in, 16)
                    act.dma_start(w2a_low[0:H1, :], w2a[D:D + H1, :]).then_inc(weights_in, 16)
                    act.dma_start(eps_col[:, :], eps.partition_broadcast(P)).then_inc(weights_in, 16)
                    act.wait_ge(diagonals_clear, 4)
                    for j in range(GROUP):
                        act.dma_start(w_msg[j * D:(j + 1) * D, j, :], w1a[0:D, :]).then_inc(diagonals_in, 16)
                        act.dma_start(w_self[j * D:(j + 1) * D, j, :], w2a[0:D, :]).then_inc(diagonals_in, 16)
                    for j in range(2):
                        act.dma_start(w_out[j * R_PAD:j * R_PAD + H2, j, :], w2b).then_inc(diagonals_in, 16)
                        act.dma_start(w_out[j * R_PAD + H2:j * R_PAD + H2C, j, :],
                                      b2b.unsqueeze(0)).then_inc(diagonals_in, 16)
                    for t in range(TILES):
                        act.dma_start(w_edge[t * D_EDGE:(t + 1) * D_EDGE, t, :], w1a[D:D + D_EDGE, :]
                                      ).then_inc(diagonals_in, 16)
                    act.dma_start(w_edge[EDGE_ROWS:EDGE_ROWS + 1, TILES - 1, :], b1a.unsqueeze(0)
                                  ).then_inc(diagonals_in, 16)
                    act.dma_start(w_edge[PICK_ROW:P, TILES - 1, :], w1a[0:D, :]).then_inc(diagonals_in, 16)
                    act.wait_ge(ln_eps_ready, 1)
                    square_and_root(act, 0, norm)
                    for step in range(1, LN_STEPS + 1):
                        for n, g in enumerate(groups_of(step - 1)):
                            if n == 2 and step < LN_STEPS:
                                square_and_root(act, step, norm)
                            copy_group(act, g, g % 2, turned, turned_copied, products)
                    act.wait_ge(weights_in, 16 * N_WEIGHTS)
                    act.wait_ge(diagonals_in, 16 * N_DIAGONALS)

                @block.gpsimd
                def _(pool):
                    nc.gpsimd.memset(w_msg[:, :, :], 0.0).then_inc(diagonals_clear, 1)
                    nc.gpsimd.memset(w_self[:, :, :], 0.0).then_inc(diagonals_clear, 1)
                    nc.gpsimd.memset(w_out[:, :, :], 0.0).then_inc(diagonals_clear, 1)
                    nc.gpsimd.memset(w_edge[:, :, :], 0.0).then_inc(diagonals_clear, 1)
                    nc.gpsimd.memset(ident[:, :], 0.0).then_inc(ident_clear, 1)
                    pool.wait_ge(ident_clear, 1)
                    nc.gpsimd.affine_select(out=ident[:, :], in_=ident[:, :], compare_op=ALU.not_equal,
                                            fill=1.0, base=0, pattern=[[-1, P]],
                                            channel_multiplier=1).then_inc(ident_ready, 1)
                    nc.gpsimd.iota(window_i[:, :], pattern=[[1, WINDOW]], base=0,
                                   channel_multiplier=0).then_inc(counted, 1)
                    nc.gpsimd.iota(piece_i[:, :], pattern=[[1, PIECES]], base=0,
                                   channel_multiplier=PIECES).then_inc(counted, 1)
                    nc.gpsimd.memset(sources[:, CHUNKS:CHUNKS + SLOTS, :], 0).then_inc(fills, 1)
                    nc.gpsimd.memset(w_mean[:, :], 0.0).then_inc(fills, 1)
                    nc.gpsimd.memset(update[:, :, :, :], 0.0).then_inc(fills, 1)
                    nc.gpsimd.memset(wide_rows[:, :], 0.0).then_inc(fills, 1)
                    pool.wait_ge(fills, 4)
                    nc.gpsimd.memset(update[:, :, :, H2:H2C], 1.0).then_inc(tail_fills, 1)
                    pool.wait_ge(tail_fills, 1)
                    nc.gpsimd.memset(w_mean[H1:SUMS, H2:H2C], 1.0).then_inc(tail_fills, 1)
                    pool.wait_ge(tail_fills, 2)
                    nc.gpsimd.memset(sums[:, :], 0.0).then_inc(tail_fills, 1)
                    for k in range(SLOTS):
                        nc.gpsimd.memset(message[k][:, :, H1:SUMS], 1.0).then_inc(tail_fills, 1)
                    pool.wait_ge(tail_fills, 3 + SLOTS)

                @block.tensor
                def _(pe):
                    pe.wait_ge(ident_ready, 1)

                    def turn(g):
                        pe.wait_ge(normed, g * GROUP // LN_BLOCKS + 1)
                        turn_group(pe, g, g % 2, turned, turned_copied)

                    turn(0)
                    for g in range(GROUPS):
                        same_step = (g + 1) % (LN_BLOCKS // GROUP) != 0
                        if same_step:
                            turn(g + 1)
                        if g == 0:
                            pe.wait_ge(diagonals_in, 16 * N_DIAGONALS)
                        pe.wait_ge(turned_copied, g + 1)
                        if g >= 2:
                            pe.wait_ge(added_msg, g - 1)
                        nc.tensor.matmul(bank[2 + g % 2][0:NP, 0:GROUP * H1], hidden_t[:, g % 2, 0:NP],
                                         w_msg[:, :, :].rearrange("p j n -> p (j n)"), start=True,
                                         stop=True).then_inc(products, 1)
                        if not same_step and g + 1 < GROUPS:
                            turn(g + 1)
                    pe.wait_ge(weights_in, 16 * N_WEIGHTS)
                    nc.tensor.matmul(bank[6][0:SUMS, 0:H2], w1b_ext_t[0:H1, :], w2a_low[0:H1, :], start=True,
                                     stop=True).then_inc(w_mean_made, 1)

                @block.vector
                def _(dve):
                    def add_bias(g):
                        dve.wait_ge(products, g + 1)
                        if g >= ROW_SLOTS:
                            dve.wait_ge(rows_out[g % ROW_SLOTS], 16 * (g // ROW_SLOTS))
                        nc.vector.tensor_tensor(projected[0:NP, g % ROW_SLOTS, :, :],
                                                bank[2 + g % 2][0:NP, 0:GROUP * H1].rearrange("p (j n) -> p j n", n=H1),
                                                spread(bias_msg[0:NP, :], GROUP, 1), ALU.add).then_inc(added_msg, 1)

                    def find_extremes(dve, k, bound, extreme):
                        dve.wait_ge(index_in, 80)
                        nc.vector.tensor_reduce(bound[0:ITERS, k:k + 1], by_iter[0:ITERS, k:k + 1, :], AX.X,
                                                extreme)

                    nc.vector.memset(ln_eps[:, :], LN_EPS).then_inc(ln_eps_ready, 1)
                    for pick in LAYER_PICKS[0]:
                        nc.vector.memset(edge_t[pick.slot][64:PICK_ROW, :], 1.0)
                    dve.wait_ge(x_in[0], 16)
                    centre(dve, 0, norm)
                    add_squares(dve, 0, norm)
                    scale(dve, 0, norm)
                    dve.wait_ge(weights_in, 16 * N_WEIGHTS)
                    for step in range(1, LN_STEPS + 1):
                        for n, g in enumerate(groups_of(step - 1)):
                            if step < LN_STEPS and n == 0:
                                dve.wait_ge(x_in[step], 16)
                                centre(dve, step, norm)
                            if step < LN_STEPS and n == 2:
                                add_squares(dve, step, norm)
                            if step >= LN_STEPS - 1:
                                find_extremes(dve, n, low if step == LN_STEPS else high,
                                              ALU.min if step == LN_STEPS else ALU.max)
                            if step < LN_STEPS and n == 3:
                                scale(dve, step, norm)
                            add_bias(g)
                    dve.wait_ge(counted, 2)
                    nc.vector.tensor_copy(window_f[:, :], window_i[:, :])
                    nc.vector.tensor_copy(piece_f[:, :], piece_i[:, :])
                    nc.vector.tensor_scalar(one_eps[:, :], eps_col[:, :], 1.0, None, ALU.add)
                    stage_first_round()
                    dve.wait_ge(w_mean_made, 1)
                    dve.wait_ge(fills, 3)
                    nc.vector.tensor_copy(w_mean[0:SUMS, 0:H2], bank[6][0:SUMS, 0:H2])

        def groups_of(step):
            per = LN_BLOCKS // GROUP
            return range(step * per, (step + 1) * per)

        def stage_first_round():
            for k in range(SLOTS):
                nc.vector.tensor_copy(index[k][:, :], sources[:, k, :])

        def gathered_rows(k, row):
            flat = gathered[k][:, :, :].rearrange("p t n -> p (t n)")[:, 0:TILES * row]
            return flat.rearrange("p (t n) -> p t n", n=row)

        def divide_sources(dve, stages, source, whole, rest, carry, block):
            nc.vector.tensor_scalar(whole, source, 1.0 / BLOCKS, 0.5 / BLOCKS - 0.5, ALU.mult,
                                    ALU.add).then_inc(stages, 1)
            dve.wait_ge(stages, 1)
            nc.vector.scalar_tensor_tensor(out=rest, in0=whole, scalar=float(-BLOCKS), in1=source,
                                           op0=ALU.mult, op1=ALU.add).then_inc(stages, 1)
            dve.wait_ge(stages, 2)
            nc.vector.tensor_scalar(carry, rest, float(BLOCKS), None, ALU.is_ge).then_inc(stages, 1)
            dve.wait_ge(stages, 3)
            nc.vector.scalar_tensor_tensor(out=block, in0=carry, scalar=float(-BLOCKS), in1=rest,
                                           op0=ALU.mult, op1=ALU.add).then_inc(stages, 1)
            dve.wait_ge(stages, 4)

        def sum_near_windows(layer):
            width, row, table = (SUMS, H1, projected_rows) if layer == 0 else (D, D, hidden_rows)
            index_ready = sem(f"index_ready{layer}")
            edge_in = [sem(f"edge_in{layer}_{k}") for k in range(SLOTS)]
            gather_in = [sem(f"gather_in{layer}_{k}") for k in range(SLOTS)]
            multiplied = sem(f"multiplied{layer}")
            added = sem(f"added{layer}")
            rectified = sem(f"rectified{layer}")
            hot = sem(f"hot{layer}")
            windows = sem(f"windows{layer}")
            summed = sem(f"summed{layer}")
            opened = sem(f"opened{layer}")
            edges_used = multiplied if layer == 0 else added
            picks = LAYER_PICKS[layer]
            NPICKS = len(picks)
            picked_slots = [pick.slot for pick in picks]
            owners_in = [sem(f"owners_in{layer}_{s}") for s in range(NPICKS)]
            owners_hot = sem(f"owners_hot{layer}")
            pieces_summed = sem(f"pieces_summed{layer}")
            pieces_placed = sem(f"pieces_placed{layer}")
            picked = sem(f"picked{layer}")
            places_hot = sem(f"places_hot{layer}")
            blocks_flat = block_in_piece[:, :, :].rearrange("p i s -> p (i s)")
            if layer == 0:
                parts = [hidden]
                owner_hot = [owner_hot_halves[:, 2 * s:2 * s + 2, :, :].rearrange("p s j e -> p (s j e)").bitcast(
                    F32).rearrange("p (j e) -> p j e", e=P) for s in range(NPICKS)]
                pick_bank = [bank[6], bank[5]]
            else:
                parts = [hidden_parts[:, part, :, :] for part in range(PARTS)]
                owner_hot = [owner_hot_halves[:, s, :, :] for s in range(PICKS)]
                pick_bank = [bank[6], bank[7], bank[0], bank[1]]
                rounded = sem("rounded")
                reduced = sem("reduced")
            piece_order = [0, PIECES - 1, *range(1, PIECES - 1)]
            products_of_a_pick = [(j, part) for j in piece_order for part in parts]
            if layer == 0:
                bound_steps = sem("bound_steps")
                bounds_ready = sem("bounds_ready")
                bounds_out = sem("bounds_out")
                bounds_in = sem("bounds_in")
                farthest = sem("farthest")
                turned = sem("turned_again")
                turned_copied = sem("turned_again_copied")
                products = sem("self_products")
                added_self = sem("added_self")
                offset_ready = sem("offset_ready")
                row_division = sem("row_division")
                column_division = sem("column_division")
                owners_ready = sem("owners_ready")
                owners_out = sem("owners_out")
                places_ready = sem("places_ready")
                picks_turned = sem("picks_turned")
                picks_copied = sem("picks_copied")

            def due(step, k):
                return [(s, pick) for s, pick in enumerate(picks) if pick._asdict()[step] == k]

            def early_ones():
                return [(s, pick) for s, pick in enumerate(picks) if pick.early]

            with nc.Block() as block:
                def exchange_bounds(sp):
                    sp.wait_ge(bounds_ready, 2)
                    sp.dma_start(base_line, low[0:ITERS, :]).then_inc(bounds_out, 16)
                    sp.dma_start(base_rows, low_i[0:ITERS, :]).then_inc(bounds_out, 16)
                    sp.dma_start(far_rows, far_n[0:ITERS, :]).then_inc(bounds_out, 16)
                    sp.wait_ge(bounds_out, 48)
                    sp.dma_start(base_all[:, :], base_line.rearrange("i s -> (i s)").partition_broadcast(P)
                                  ).then_inc(bounds_in, 16)
                    sp.dma_start(bases[:, :], base_rows.rearrange("i s -> (i s)").unsqueeze(0)
                                  ).then_inc(bounds_in, 16)
                    sp.dma_start(fars[:, :], far_rows.rearrange("i s -> (i s)").unsqueeze(0)
                                  ).then_inc(bounds_in, 16)

                @block.sync
                def _(sp):
                    if layer == 0:
                        exchange_bounds(sp)
                        sp.wait_ge(owners_ready, 1)
                        sp.dma_start(owner_rows, owner[0:ITERS + 1, :, :]).then_inc(owners_out, 16)
                        sp.wait_ge(owners_out, 16)
                    def load_owners(s, pick, i):
                        sp.wait_ge(owners_hot, NPICKS * i + (s + 1))
                        row_of = PICK_SLOTS.index(pick.slot)
                        sp.dma_start(owner_in[s][:, :], owner_rows[bass.ds(i, 1), row_of, :].rearrange(
                            "o e -> (o e)").partition_broadcast(P)).then_inc(owners_in[s], 16)

                    for s, pick in early_ones():
                        load_owners(s, pick, 0)
                    with sp.Fori(0, ITERS) as i:
                        for k in range(SLOTS):
                            for s, pick in due("find", k):
                                load_owners(s, pick, i + pick.early)
                            sp.wait_ge(edges_used, SLOTS * i + (k + 1))
                            if layer == 0:
                                sp.dma_start(edge_t[k][0:EDGE_ROWS, :], edge16[bass.ds(SLOTS * i + k, 1), :, :].rearrange(
                                    "o d e -> (o d) e")).then_inc(edge_in[k], 16)
                            else:
                                sp.dma_start(edge_r[k][:, :, :],
                                             edge32[bass.ds(SLOTS * i + k, 1), :, :, :].rearrange(
                                                 "o p t d -> (o p) t d")).then_inc(edge_in[k], 16)

                @block.gpsimd
                def _(pool):
                    with pool.Fori(0, ITERS) as i:
                        for k in range(SLOTS):
                            pool.wait_ge(index_ready, SLOTS * i + (k + 1))
                            pool.wait_ge(rectified, SLOTS * i + (k + 1))
                            pool.sem_inc(opened, 1)
                            for t in range(TILES - (k in picked_slots)):
                                pool.indirect_dma_start(
                                    gathered_rows(k, row)[:, t, :], None, table,
                                    bass.IndirectOffsetOnAxis(ap=index[k][:, t:t + 1], axis=0)
                                ).then_inc(gather_in[k], 16)

                def self_products(pe):
                    turn_group(pe, 0, 4, turned, turned_copied)
                    for g in range(GROUPS):
                        if g + 1 < GROUPS:
                            turn_group(pe, g + 1, 4 + (g + 1) % 2, turned, turned_copied)
                        pe.wait_ge(turned_copied, g + 1)
                        if g >= 2:
                            pe.wait_ge(added_self, g - 1)
                        nc.tensor.matmul(bank[6 + g % 2][0:NP, 0:GROUP * H2], hidden_t[:, g % 2, 0:NP],
                                         w_self[:, :, :].rearrange("p j n -> p (j n)"), start=True,
                                         stop=True).then_inc(products, 1)

                def find_bounds(dve):
                    nc.vector.memset(low_i[:, :], 0).then_inc(bound_steps, 1)
                    nc.vector.memset(far_n[:, :], 0).then_inc(bound_steps, 1)
                    dve.wait_ge(bound_steps, 2)
                    nc.vector.tensor_copy(low_i[0:ITERS, 0:SLOTS], low[0:ITERS, :]).then_inc(bounds_ready, 1)
                    nc.vector.tensor_tensor(far_i[0:ITERS, 0:SLOTS], high[0:ITERS, :], low[0:ITERS, :],
                                            ALU.subtract).then_inc(bound_steps, 1)
                    dve.wait_ge(bound_steps, 3)
                    nc.vector.tensor_single_scalar(far_n[0:ITERS, 0:SLOTS], far_i[0:ITERS, 0:SLOTS],
                                                   WINDOW_BITS, ALU.arith_shift_right).then_inc(bounds_ready, 1)

                def add_self_bias(dve):
                    for g in range(GROUPS):
                        dve.wait_ge(products, g + 1)
                        nc.vector.tensor_tensor(self_part[0:NP, g * GROUP:(g + 1) * GROUP, :],
                                                bank[6 + g % 2][0:NP, 0:GROUP * H2].rearrange("p (j n) -> p j n", n=H2),
                                                spread(bias_self[0:NP, :], GROUP, 1), ALU.add).then_inc(added_self, 1)

                def find_owner_rows(dve):
                    rows = slice(0, ITERS + 1)
                    divide_sources(dve, row_division, pick_source[rows, :, :], row_whole[rows, :, :],
                                   row_rest[rows, :, :], row_carry[rows, :, :], row_block[rows, :, :])
                    nc.vector.tensor_tensor(row_rest[rows, :, :], row_whole[rows, :, :], row_carry[rows, :, :],
                                            ALU.add).then_inc(row_division, 1)
                    nc.vector.tensor_single_scalar(row_block[rows, :, :], row_block[rows, :, :], PIECE_BITS,
                                                   ALU.arith_shift_right).then_inc(row_division, 1)
                    dve.wait_ge(row_division, 6)
                    nc.vector.scalar_tensor_tensor(out=owner[rows, :, :], in0=row_rest[rows, :, :],
                                                   scalar=float(PIECES), in1=row_block[rows, :, :],
                                                   op0=ALU.mult, op1=ALU.add).then_inc(owners_ready, 1)

                def find_places(dve):
                    columns = sources[:, 0:CHUNKS + SLOTS, TILES - 1:TILES].rearrange("p (i k) o -> p i (k o)", k=SLOTS)
                    columns = columns[:, :, PICK_SLOTS[0]:PICK_SLOTS[-1] + 1]
                    dve.wait_ge(owners_ready, 1)
                    divide_sources(dve, column_division, columns, column_whole, column_rest, column_carry,
                                   column_block)
                    nc.vector.tensor_single_scalar(block_in_piece[:, :, :], column_block, PIECE - 1,
                                                   ALU.bitwise_and).then_inc(places_ready, 1)
                    dve.wait_ge(places_ready, 1)

                def split_hidden(dve):
                    dve.wait_ge(rounded, 1)
                    nc.vector.tensor_tensor(hidden[0:NP, :, :], hidden[0:NP, :, :], hidden_parts[0:NP, 0, :, :],
                                            ALU.subtract).then_inc(reduced, 1)
                    dve.wait_ge(rounded, 2)
                    nc.vector.tensor_tensor(hidden_parts[0:NP, 2, :, :], hidden[0:NP, :, :],
                                            hidden_parts[0:NP, 1, :, :], ALU.subtract).then_inc(reduced, 1)

                def round_hidden(act):
                    nc.scalar.copy(hidden_parts[0:NP, 0, :, :], hidden[0:NP, :, :]).then_inc(rounded, 1)
                    act.wait_ge(reduced, 1)
                    nc.scalar.copy(hidden_parts[0:NP, 1, :, :], hidden[0:NP, :, :]).then_inc(rounded, 1)

                def find_offsets(dve):
                    dve.wait_ge(bounds_in, 48)
                    nc.vector.tensor_tensor(offsets, destinations[:, :, :],
                                            spread(base_all[:, :], TILES, 2), ALU.subtract).then_inc(offset_ready, 1)
                    nc.vector.tensor_reduce(far_max[:, :], fars[:, :], AX.X, ALU.max).then_inc(farthest, 1)
                    dve.wait_ge(farthest, 1)
                    nc.vector.tensor_copy(far_flag[:, :], far_max[:, :])
                    dve.wait_ge(offset_ready, 1)

                @block.tensor
                def _(pe):
                    if layer == 0:
                        pe.sem_inc(multiplied, SLOTS)
                        pe.sem_inc(picks_turned, 1)
                    pe.sem_inc(windows, SLOTS)
                    pe.sem_inc(pieces_summed, NPICKS)
                    if layer == 0:
                        self_products(pe)
                        pe.wait_ge(added_self, GROUPS)
                    else:
                        pe.wait_ge(rounded, 2)
                        pe.wait_ge(reduced, 2)

                    def sum_pieces(s, i):
                        pe.wait_ge(owners_hot, NPICKS * i + (s + NPICKS + 1))
                        pe.wait_ge(pieces_placed, NPICKS * i + (s + 1))
                        for n, (j, part) in enumerate(products_of_a_pick):
                            b = slice(j * PIECE, min((j + 1) * PIECE, BLOCKS))
                            last = nc.tensor.matmul(
                                pick_bank[s][:, 0:(b.stop - b.start) * D], owner_hot[s][0:NP, j, :],
                                part[0:NP, b, :].rearrange("p b f -> p (b f)"),
                                start=(n == 0), stop=(n == len(products_of_a_pick) - 1))
                        last.then_inc(pieces_summed, 1)

                    for s, pick in early_ones():
                        sum_pieces(s, 0)
                    with pe.Fori(0, ITERS) as i:
                        def edge_products(k):
                            pe.wait_ge(edge_in[k], 16 * i + 16)
                            pe.wait_ge(added, SLOTS * i + (k + SLOTS - 1))
                            rows = EDGE_ROWS
                            if k in picked_slots:
                                pe.wait_ge(picks_copied, NPICKS * i + (picked_slots.index(k) + 2))
                                rows = P
                            nc.tensor.matmul(bank[k % 3][:, 0:TILES * H1], edge_t[k][0:rows, :],
                                             w_edge[0:rows, :, :].rearrange("p t n -> p (t n)"),
                                             start=True, stop=True).then_inc(multiplied, 1)

                        if layer == 0:
                            edge_products(0)
                        for k in range(SLOTS):
                            if layer == 0:
                                for s, pick in due("pick", k):
                                    pe.wait_ge(picked, NPICKS * i + (s + NPICKS + 1))
                                    pe.wait_ge(picks_copied, NPICKS * i + (s + 1))
                                    nc.tensor.transpose(bank[7][:, 0:P], wide_rows[:, :], ident[:, :]
                                                        ).then_inc(picks_turned, 1)
                                if k + 1 < SLOTS:
                                    edge_products(k + 1)
                            pe.wait_ge(rectified, SLOTS * i + (k + SLOTS + 1))
                            pe.wait_ge(hot, SLOTS * i + (k + 1))
                            pe.wait_ge(summed, SLOTS * i + (k + 1 + (k == 0)))
                            for t in range(TILES):
                                last = nc.tensor.matmul(bank[3 + k % 2][0:width, 0:WINDOW],
                                                        message[k][:, t, 0:width], onehot[k][:, t, :],
                                                        start=(t == 0), stop=(t == TILES - 1))
                            last.then_inc(windows, 1)
                            for s, pick in due("sum", k):
                                sum_pieces(s, i + pick.early)

                @block.scalar
                def _(act):
                    act.sem_inc(rectified, SLOTS)
                    if layer == 0:
                        act.sem_inc(picks_copied, 1)
                        for g in range(GROUPS):
                            copy_group(act, g, 4 + g % 2, turned, turned_copied, products)
                    else:
                        round_hidden(act)
                    with act.Fori(0, ITERS) as i:
                        for k in range(SLOTS):
                            for s, pick in due("pick", k) if layer == 0 else ():
                                act.wait_ge(picks_turned, NPICKS * i + (s + 2))
                                act.wait_ge(multiplied, SLOTS * i + (pick.slot + 1))
                                nc.scalar.copy(edge_t[pick.slot][PICK_ROW:P, :], bank[7][PICK_ROW:P, 0:P]
                                               ).then_inc(picks_copied, 1)
                            act.wait_ge(added, SLOTS * i + (k + SLOTS + 1))
                            act.wait_ge(windows, SLOTS * i + (k + 1))
                            nc.scalar.activation(message[k][:, :, 0:row], gathered_rows(k, row),
                                                 ACT.Relu).then_inc(rectified, 1)

                @block.vector
                def _(dve):
                    dve.sem_inc(added, SLOTS)
                    dve.sem_inc(summed, 2)
                    dve.sem_inc(index_ready, SLOTS)
                    dve.sem_inc(owners_hot, NPICKS)
                    dve.sem_inc(pieces_placed, NPICKS)
                    dve.sem_inc(picked, NPICKS)
                    if layer == 0:
                        find_bounds(dve)
                        find_owner_rows(dve)
                        add_self_bias(dve)
                        find_offsets(dve)
                        find_places(dve)
                    else:
                        nc.vector.scalar_tensor_tensor(out=nodes[0:NP, :, :], in0=hidden[0:NP, :, :],
                                                       scalar=one_eps[0:NP, 0:1], in1=nodes[0:NP, :, :],
                                                       op0=ALU.mult, op1=ALU.add)
                        split_hidden(dve)

                    def find_owners(s, pick, i):
                        column = PICKS * i + PICK_SLOTS.index(pick.slot)
                        dve.wait_ge(owners_in[s], 16 * i + 16)
                        dve.wait_ge(pieces_summed, NPICKS * i + (s + 1))
                        dve.wait_ge(pieces_placed, NPICKS * i + (s + 1))
                        nc.vector.tensor_tensor(place_hot[s][:, :], window_f[:, 0:PIECE],
                                                blocks_flat[:, bass.ds(column, 1)].broadcast_to([P, PIECE]),
                                                ALU.is_equal).then_inc(places_hot, 1)
                        nc.vector.tensor_tensor(owner_hot[s][0:NP, :, :], spread(owner_in[s][0:NP, :], PIECES, 1),
                                                spread(piece_f[0:NP, :], P, 2), ALU.is_equal
                                                ).then_inc(owners_hot, 1)

                    for s, pick in early_ones():
                        find_owners(s, pick, 0)
                    with dve.Fori(0, ITERS) as i:
                        def add_window(k, base):
                            dve.wait_ge(windows, SLOTS * i + (k + SLOTS + 1))
                            dve.wait_ge(summed, SLOTS * i + (k + 2))
                            nc.vector.tensor_tensor(sums[0:width, bass.ds(base, WINDOW)],
                                                    sums[0:width, bass.ds(base, WINDOW)],
                                                    bank[3 + k % 2][0:width, 0:WINDOW],
                                                    ALU.add).then_inc(summed, 1)

                        def pick_rows(s, pick):
                            dve.wait_ge(pieces_summed, NPICKS * i + (s + NPICKS + 1))
                            dve.wait_ge(places_hot, NPICKS * i + (s + 1))
                            dve.wait_ge(picked, NPICKS * i + (s + NPICKS))
                            nc.vector.tensor_tensor(placed_rows[:, :, :],
                                                    pick_bank[s][:, 0:PIECE * D].rearrange("p (b f) -> p b f", f=D),
                                                    spread(place_hot[s][:, :], D, 2),
                                                    ALU.mult).then_inc(pieces_placed, 1)
                            dve.wait_ge(pieces_placed, NPICKS * i + (s + NPICKS + 1))
                            if layer == 0:
                                dve.wait_ge(picks_turned, NPICKS * i + (s + 1))
                                rows = wide_rows[:, PICK_ROW:P]
                            else:
                                dve.wait_ge(rectified, SLOTS * i + (pick.slot + 1))
                                rows = gathered_rows(pick.slot, row)[:, TILES - 1, :]
                            nc.vector.tensor_reduce(rows, placed_rows[:, :, :].rearrange("p b f -> p f b"),
                                                    AX.X, ALU.add).then_inc(picked, 1)
                            if layer:
                                dve.wait_ge(picked, NPICKS * i + (s + NPICKS + 1))

                        base_of = []
                        for k in range(SLOTS):
                            for s, pick in due("find", k):
                                find_owners(s, pick, i + pick.early)
                            for s, pick in due("pick", k):
                                pick_rows(s, pick)
                            base_of.append(dve.value_load(bases[0:1, bass.ds(ROW_PAD * i + k, 1)], min_val=0,
                                                          max_val=N - 1))
                            dve.wait_ge(windows, SLOTS * i + (k + 1))
                            nc.vector.tensor_tensor(
                                onehot[k][:, :, :], spread(window_f[:, :], TILES, 1),
                                spread(offsets[:, bass.ds(SLOTS * i + k, 1), :].rearrange("p o t -> p (o t)"),
                                       WINDOW, 2), ALU.is_equal).then_inc(hot, 1)
                            tiles_in = TILES - (k in picked_slots)
                            dve.wait_ge(gather_in[k], 16 * tiles_in * i + 16 * tiles_in)
                            if layer == 0:
                                dve.wait_ge(multiplied, SLOTS * i + (k + SLOTS + 1))
                                other = bank[k % 3][:, 0:TILES * H1].rearrange("p (t n) -> p t n", n=H1)
                            else:
                                dve.wait_ge(edge_in[k], 16 * i + 16)
                                other = edge_r[k][:, :, :]
                            tiles_added = TILES
                            if layer == 0 and k in picked_slots:
                                tiles_added = TILES - 1
                                nc.vector.tensor_copy(gathered_rows(k, row)[:, tiles_added, :],
                                                      other[:, tiles_added, :])
                            some_rows = gathered_rows(k, row)[:, 0:tiles_added, :]
                            nc.vector.tensor_tensor(some_rows, some_rows, other[:, 0:tiles_added, :],
                                                    ALU.add).then_inc(added, 1)
                            nc.vector.tensor_copy(
                                index[k][:, :],
                                sources[:, bass.ds(SLOTS * i + (k + SLOTS), 1), :].rearrange("p o t -> p (o t)")
                            ).then_inc(index_ready, 1)
                            if k:
                                add_window(k - 1, base_of[k - 1])
                        add_window(SLOTS - 1, base_of[SLOTS - 1])

        def sum_far_windows(layer):
            width, row, table = (SUMS, H1, projected_rows) if layer == 0 else (D, D, hidden_rows)
            staged = sem(f"far_staged{layer}")
            edge_in = sem(f"far_edge_in{layer}")
            gather_in = [sem(f"far_gather_in{layer}_{k}") for k in range(SLOTS)]
            multiplied = sem(f"far_multiplied{layer}")
            added = sem(f"far_added{layer}")
            moved = sem(f"far_moved{layer}")
            hot = sem(f"far_hot{layer}")
            window = sem(f"far_window{layer}")

            def clear(*used):
                for s in used:
                    nc.sync.sem_clear(s)
                nc.all_engine_barrier()

            def chunk_messages(i, k):
                chunk = SLOTS * i + k

                with nc.Block() as block:
                    @block.sync
                    def _(sp):
                        if layer == 0:
                            sp.dma_start(edge_t[0][0:EDGE_ROWS, :], edge16[bass.ds(chunk, 1), :, :].rearrange(
                                "o d e -> (o d) e")).then_inc(edge_in, 16)
                        else:
                            sp.dma_start(edge_r[0][:, :, :], edge32[bass.ds(chunk, 1), :, :, :].rearrange(
                                "o p t d -> (o p) t d")).then_inc(edge_in, 16)

                    @block.gpsimd
                    def _(pool):
                        pool.wait_ge(staged, 1)
                        for t in range(TILES):
                            pool.indirect_dma_start(
                                gathered_rows(0, row)[:, t, :], None, table,
                                bass.IndirectOffsetOnAxis(ap=index[0][:, t:t + 1], axis=0)
                            ).then_inc(gather_in[k], 16)

                    @block.tensor
                    def _(pe):
                        if layer == 0:
                            pe.wait_ge(edge_in, 16)
                            nc.tensor.matmul(bank[0][:, 0:TILES * H1], edge_t[0][0:EDGE_ROWS, :],
                                             w_edge[0:EDGE_ROWS, :, :].rearrange("p t n -> p (t n)"),
                                             start=True, stop=True).then_inc(multiplied, 1)

                    @block.scalar
                    def _(act):
                        act.wait_ge(added, 1)
                        nc.scalar.activation(message[0][:, :, 0:row], gathered_rows(0, row), ACT.Relu)

                    @block.vector
                    def _(dve):
                        nc.vector.tensor_copy(index[0][:, :], sources[:, bass.ds(chunk, 1), :].rearrange(
                            "p o t -> p (o t)")).then_inc(staged, 1)
                        nc.vector.tensor_copy(far_offset[:, :], offsets[:, bass.ds(chunk, 1), :].rearrange(
                            "p o t -> p (o t)"))
                        dve.wait_ge(gather_in[k], 16 * TILES * i + 16 * TILES)
                        if layer == 0:
                            dve.wait_ge(multiplied, 1)
                            other = bank[0][:, 0:TILES * H1].rearrange("p (t n) -> p t n", n=H1)
                        else:
                            dve.wait_ge(edge_in, 16)
                            other = edge_r[0][:, :, :]
                        nc.vector.tensor_tensor(gathered_rows(0, row), gathered_rows(0, row), other,
                                                ALU.add).then_inc(added, 1)
                clear(staged, edge_in, multiplied, added)

            def add_window(base, w):
                with nc.Block() as block:
                    @block.vector
                    def _(dve):
                        nc.vector.tensor_scalar(far_offset[:, :], far_offset[:, :], float(-WINDOW), None,
                                                ALU.add).then_inc(moved, 1)
                        dve.wait_ge(moved, 1)
                        nc.vector.tensor_tensor(onehot[0][:, :, :], spread(window_f[:, :], TILES, 1),
                                                spread(far_offset[:, :], WINDOW, 2), ALU.is_equal).then_inc(hot, 1)
                        dve.wait_ge(window, 1)
                        first = nc.s_assert_within(base + w * WINDOW, 0, N - 1 + WINDOW)
                        nc.vector.tensor_tensor(sums[0:width, bass.ds(first, WINDOW)],
                                                sums[0:width, bass.ds(first, WINDOW)],
                                                bank[3][0:width, 0:WINDOW], ALU.add)

                    @block.tensor
                    def _(pe):
                        pe.wait_ge(hot, 1)
                        for t in range(TILES):
                            last = nc.tensor.matmul(bank[3][0:width, 0:WINDOW], message[0][:, t, 0:width],
                                                    onehot[0][:, t, :], start=(t == 0), stop=(t == TILES - 1))
                        last.then_inc(window, 1)
                clear(moved, hot, window)

            some = nc.values_load(far_flag[0:1, 0:1], min_val=0, max_val=N)
            with nc.If(some > 0):
                with nc.Fori(0, ITERS) as i:
                    for k in range(SLOTS):
                        chunk_messages(i, k)
                        base = nc.values_load(bases[0:1, bass.ds(ROW_PAD * i + k, 1)], min_val=0, max_val=N - 1)
                        last = nc.values_load(fars[0:1, bass.ds(ROW_PAD * i + k, 1)], min_val=0,
                                              max_val=(N - 1) // WINDOW)
                        with nc.Fori(1, last + 1) as w:
                            add_window(base, w)


        def update_nodes():
            norm = norm_semaphores(1)
            normed = norm["normed"]
            means = sem("means")
            capped = sem("capped")
            inverted = sem("inverted_counts")
            scaled = sem("scaled")
            shifted = sem("shifted")
            updates = sem("updates")
            turned = sem("turned1")
            turned_copied = sem("turned_copied1")
            outputs = sem("outputs")
            advanced = sem("advanced")
            hidden_out = sem("hidden_out")
            cleared = sem("cleared")
            PER_STEP = LN_BLOCKS // BATCH
            TURN, OUTPUT = AHEAD, AHEAD + 2

            def blocks(q):
                return slice(q * BATCH, (q + 1) * BATCH)

            with nc.Block() as block:
                @block.tensor
                def _(pe):
                    def mean(q):
                        if q >= AHEAD:
                            pe.wait_ge(scaled, q - AHEAD + 1)
                        for j in range(BATCH):
                            last = nc.tensor.matmul(bank[q % AHEAD][0:NP, j * H2C:(j + 1) * H2C],
                                                    sums[0:SUMS, q * BATCH + j:N:BLOCKS], w_mean[0:SUMS, :],
                                                    start=True, stop=True)
                        last.then_inc(means, 1)

                    def turn(q):
                        pe.wait_ge(updates, q + 1)
                        if q >= 2:
                            pe.wait_ge(turned_copied, q - 1)
                        for j in range(PAIRS):
                            last = nc.tensor.transpose(
                                bank[TURN + q % 2][:, j * NP:(j + 1) * NP],
                                update[0:NP, q % AHEAD, 2 * j:2 * j + 2, :].rearrange("p b f -> p (b f)"),
                                ident[0:NP, 0:NP])
                        last.then_inc(turned, 1)

                    for q in range(AHEAD):
                        mean(q)
                    turn(0)
                    for q in range(BATCHES):
                        if q + 1 < BATCHES:
                            turn(q + 1)
                        pe.wait_ge(turned_copied, q + 1)
                        if q >= 2:
                            pe.wait_ge(advanced, q - 1)
                        for j in range(PAIRS):
                            last = nc.tensor.matmul(bank[OUTPUT + q % 2][0:NP, j * 2 * D:(j + 1) * 2 * D],
                                                    update_t[:, q % 2, j, 0:NP],
                                                    w_out[:, :, :].rearrange("p j n -> p (j n)"),
                                                    start=True, stop=True)
                        last.then_inc(outputs, 1)
                        if q + AHEAD < BATCHES:
                            mean(q + AHEAD)

                @block.scalar
                def _(act):
                    def rectify(q):
                        act.wait_ge(shifted, q + 1)
                        nc.scalar.activation(update[0:NP, q % AHEAD, :, 0:H2], update[0:NP, q % AHEAD, :, 0:H2],
                                             ACT.Relu).then_inc(updates, 1)

                    rectify(0)
                    for q in range(BATCHES):
                        if q + 1 < BATCHES:
                            rectify(q + 1)
                        act.wait_ge(turned, q + 1)
                        if q >= 2:
                            act.wait_ge(outputs, q - 1)
                        nc.scalar.copy(update_t[:, q % 2, :, 0:NP],
                                       bank[TURN + q % 2][:, 0:PAIRS * NP].rearrange("p (j n) -> p j n", n=NP)
                                       ).then_inc(turned_copied, 1)
                        if q % PER_STEP == 1 and q > 1:
                            square_and_root(act, q // PER_STEP - 1, norm)
                    square_and_root(act, LN_STEPS - 1, norm)

                @block.vector
                def _(dve):
                    def first_layer(q):
                        s = q % AHEAD
                        dve.wait_ge(means, q + 1)
                        view = bank[s][0:NP, 0:BATCH * H2C].rearrange("p (b n) -> p b n", n=H2C)
                        count = view[:, :, H2:H2C].rearrange("p b o -> p (b o)")
                        nc.vector.tensor_scalar(inverse[0:NP, 0, :], count, 1.0, None, ALU.max).then_inc(capped, 1)
                        dve.wait_ge(capped, q + 1)
                        nc.vector.reciprocal(inverse[0:NP, 1, :], inverse[0:NP, 0, :]).then_inc(inverted, 1)
                        dve.wait_ge(inverted, q + 1)
                        if q >= AHEAD:
                            dve.wait_ge(turned, q - AHEAD + 1)
                        nc.vector.tensor_tensor(update[0:NP, s, :, 0:H2], view[:, :, 0:H2],
                                                spread(inverse[0:NP, 1, :], H2, 2), ALU.mult).then_inc(scaled, 1)
                        dve.wait_ge(scaled, q + 1)
                        nc.vector.tensor_tensor(update[0:NP, s, :, 0:H2], update[0:NP, s, :, 0:H2],
                                                self_part[0:NP, blocks(q), :], ALU.add).then_inc(shifted, 1)

                    stage_first_round()
                    first_layer(0)
                    first_layer(1)
                    for q in range(BATCHES):
                        if q + 2 < BATCHES:
                            first_layer(q + 2)
                        dve.wait_ge(outputs, q + 1)
                        nc.vector.tensor_tensor(nodes[0:NP, blocks(q), :], nodes[0:NP, blocks(q), :],
                                                bank[OUTPUT + q % 2][0:NP, 0:BATCH * D].rearrange(
                                                    "p (b n) -> p b n", n=D), ALU.add).then_inc(advanced, 1)
                        step = q // PER_STEP - 1
                        if step >= 0 and q % PER_STEP == 1:
                            add_squares(dve, step, norm)
                        if step >= 0 and q % PER_STEP == 2:
                            scale(dve, step, norm)
                        if q % PER_STEP == PER_STEP - 1:
                            dve.wait_ge(advanced, q + 1)
                            centre(dve, q // PER_STEP, norm)
                    add_squares(dve, LN_STEPS - 1, norm)
                    scale(dve, LN_STEPS - 1, norm)

                @block.sync
                def _(sp):
                    for step in range(LN_STEPS):
                        sp.wait_ge(normed, step + 1)
                        sp.dma_start(hidden_view[:, ln_blocks(step), :],
                                     hidden[0:NP, ln_blocks(step), :]).then_inc(hidden_out, 16)
                    sp.wait_ge(hidden_out, 16 * LN_STEPS)

                @block.gpsimd
                def _(pool):
                    pool.wait_ge(means, BATCHES)
                    nc.gpsimd.memset(sums[0:D, :], 0.0).then_inc(cleared, 1)
                    pool.wait_ge(cleared, 1)

        def finish():
            turned = sem("turned2")
            joined = sem("joined")
            stored = sem("stored")
            with nc.Block() as block:
                @block.tensor
                def _(pe):
                    for q in range(OUT_BATCHES):
                        if q >= 8:
                            pe.wait_ge(joined, q - 7)
                        for j in range(OUT_BATCH):
                            last = nc.tensor.transpose(bank[q % 8][0:NP, j * D:(j + 1) * D],
                                                       sums[0:D, q * OUT_BATCH + j:N:BLOCKS], ident[0:D, 0:D])
                        last.then_inc(turned, 1)

                @block.vector
                def _(dve):
                    for q in range(OUT_BATCHES):
                        b = slice(q * OUT_BATCH, (q + 1) * OUT_BATCH)
                        dve.wait_ge(turned, q + 1)
                        nc.vector.tensor_tensor(nodes[0:NP, b, :], nodes[0:NP, b, :],
                                                bank[q % 8][0:NP, 0:OUT_BATCH * D].rearrange("p (b n) -> p b n", n=D),
                                                ALU.add).then_inc(joined, 1)

                @block.sync
                def _(sp):
                    for q in range(OUT_BATCHES):
                        b = slice(q * OUT_BATCH, (q + 1) * OUT_BATCH)
                        sp.wait_ge(joined, q + 1)
                        sp.dma_start(out_view[:, b, :], nodes[0:NP, b, :]).then_inc(stored, 16)
                    sp.wait_ge(stored, 16 * OUT_BATCHES)

        prepare()
        sum_near_windows(0)
        sum_far_windows(0)
        update_nodes()
        sum_near_windows(1)
        sum_far_windows(1)
        finish()


def kernel(**inputs):
    import numpy as _np
    import concourse.bacc as _bacc
    from concourse import mybir as _mybir
    from concourse.bass_utils import run_bass_kernel_spmd as _run

    a = {k: _np.ascontiguousarray(v) for k, v in inputs.items()}
    chunks = a["src"].shape[0] // CHUNK
    arrays = {
        "x": a["x"],
        "src_cols": a["src"].reshape(chunks, P, TILES).transpose(1, 0, 2),
        "src_picks": a["src"].reshape(chunks // SLOTS, SLOTS, P, TILES)[..., TILES - 1][:, list(PICK_SLOTS)],
        "dst_cols": a["dst"].reshape(chunks, P, TILES).transpose(1, 0, 2),
        "dst_rows": a["dst"].reshape(chunks // SLOTS, SLOTS, CHUNK),
        "edge16": a["edge_attr_16"].reshape(chunks, P, TILES, -1).transpose(0, 2, 3, 1).reshape(chunks, -1, P),
        "edge32": a["edge_attr_32"].reshape(chunks, P, TILES, -1),
        "w1a": a["L0_gnn_w1a"], "b1a": a["L0_gnn_b1a"], "w1b_t": a["L0_gnn_w1b"].T, "b1b": a["L0_gnn_b1b"],
        "w2a": a["L0_gnn_w2a"], "b2a": a["L0_gnn_b2a"], "w2b": a["L0_gnn_w2b"], "b2b": a["L0_gnn_b2b"],
        "eps": a["L1_gnn_eps"],
    }
    arrays = {k: _np.ascontiguousarray(v) for k, v in arrays.items()}
    nc = _bacc.Bacc("TRN2", target_bir_lowering=False, num_devices=1)
    args = [nc.dram_tensor(f"in_{k}", v.shape, _mybir.dt.from_np(v.dtype), kind="ExternalInput").ap()
            for k, v in arrays.items()]
    out = nc.dram_tensor("out_0", a["x"].shape, F32, kind="ExternalOutput").ap()
    gnn_kernel(nc, *args, out)
    r = _run(nc, [{f"in_{k}": v for k, v in arrays.items()}], core_ids=[0])
    return r.results[0]["out_0"]
```
